# Optimizing a Trainium2 kernel written in Bass

```python
import numpy as np
import jax
import jax.numpy as jnp

def _softmax(x, axis=-1):
    return jax.nn.softmax(x, axis=axis)

def _gelu(x):
    return jax.nn.gelu(x, approximate=True)

def _silu(x):
    return jax.nn.silu(x)

def _sigmoid(x):
    return jax.nn.sigmoid(x)

def _layernorm(x, axis=-1, eps=1e-05):
    m = jnp.mean(x, axis=axis, keepdims=True)
    v = jnp.var(x, axis=axis, keepdims=True)
    return (x - m) / jnp.sqrt(v + eps)

def _scatter_add(tgt, idx, src, axis=0):
    return tgt.at[idx].add(src)

def _segment_sum(src, seg, n):
    return jax.ops.segment_sum(src, seg, n)
kernel_name = 'mk_macaron_d1_jaxref_r8_b58ce0'

def setup_inputs(seed: int=0):
    np.random.seed(seed)
    _w = jnp.asarray

    def _L0_attn_setup():
        import jax, jax.numpy as jnp
        import numpy as np
        D_MODEL, N_HEADS, N_KV, HEAD_DIM, D_LAT = (128, 8, 2, 128, 32)
        N_REP = N_HEADS // N_KV
        B, T = (2, 256)
        key = jax.random.key(seed)
        ks = jax.random.split(key, 8)
        s = lambda fan_in: 1.0 / np.sqrt(fan_in)
        return {'x': jax.random.normal(ks[0], (B, T, D_MODEL), jnp.float32), 'wq': jax.random.normal(ks[1], (D_MODEL, N_HEADS * HEAD_DIM), jnp.float32) * s(D_MODEL), 'wk_down': jax.random.normal(ks[2], (D_MODEL, N_KV * D_LAT), jnp.float32) * s(D_MODEL), 'wv_down': jax.random.normal(ks[3], (D_MODEL, N_KV * D_LAT), jnp.float32) * s(D_MODEL), 'wk_up': jax.random.normal(ks[4], (D_LAT, HEAD_DIM), jnp.float32) * s(D_LAT), 'wv_up': jax.random.normal(ks[5], (D_LAT, HEAD_DIM), jnp.float32) * s(D_LAT), 'wo': jax.random.normal(ks[6], (N_HEADS * HEAD_DIM, D_MODEL), jnp.float32) * s(N_HEADS * HEAD_DIM)}
    _L0_attn_in = _L0_attn_setup()

    def _L0_ffn_setup():
        import jax, jax.numpy as jnp
        import numpy as np
        TOP_K = 2
        EPS = 1e-10
        key = jax.random.key(seed)
        k1, k2, k3, k4 = jax.random.split(key, 4)
        B, S, H, E = (4, 256, 128, 8)
        tokens = jax.random.normal(k1, (B, S, H), dtype=jnp.float32)
        router_w = jax.random.normal(k2, (E, H), dtype=jnp.float32) * (1.0 / np.sqrt(H))
        router_b = jax.random.normal(k3, (E,), dtype=jnp.float32) * 0.01
        expert_weights = jax.random.normal(k4, (E, H, H), dtype=jnp.float32) * (1.0 / np.sqrt(H))
        return {'tokens': tokens, 'router_w': router_w, 'router_b': router_b, 'expert_weights': expert_weights}
    _L0_ffn_in = _L0_ffn_setup()
    _d = {'L0_attn_x': _L0_attn_in['x'], 'L0_attn_wq': _L0_attn_in['wq'], 'L0_attn_wk_down': _L0_attn_in['wk_down'], 'L0_attn_wv_down': _L0_attn_in['wv_down'], 'L0_attn_wk_up': _L0_attn_in['wk_up'], 'L0_attn_wv_up': _L0_attn_in['wv_up'], 'L0_attn_wo': _L0_attn_in['wo'], 'L0_ffn_router_w': _L0_ffn_in['router_w'], 'L0_ffn_router_b': _L0_ffn_in['router_b'], 'L0_ffn_expert_weights': _L0_ffn_in['expert_weights']}
    _x0 = _d['L0_attn_x']
    _d['L0_attn_x'] = jax.random.normal(jax.random.fold_in(jax.random.key(seed), 1), (4, 1024, 128), dtype=_x0.dtype)
    del _x0
    return _d

def reference(L0_attn_x, L0_attn_wq, L0_attn_wk_down, L0_attn_wv_down, L0_attn_wk_up, L0_attn_wv_up, L0_attn_wo, L0_ffn_router_w, L0_ffn_router_b, L0_ffn_expert_weights):

    def _L0_attn_ref(x, wq, wk_down, wv_down, wk_up, wv_up, wo):
        import jax, jax.numpy as jnp
        import numpy as np
        D_MODEL, N_HEADS, N_KV, HEAD_DIM, D_LAT = (128, 8, 2, 128, 32)
        N_REP = N_HEADS // N_KV
        B, T = (2, 256)
        Bq, Tq, _ = x.shape
        scale = HEAD_DIM ** (-0.5)
        q = (x @ wq).reshape(Bq, Tq, N_KV, N_REP, HEAD_DIM)
        k_lat = (x @ wk_down).reshape(Bq, Tq, N_KV, D_LAT)
        v_lat = (x @ wv_down).reshape(Bq, Tq, N_KV, D_LAT)
        k = jnp.einsum('bkhl,ld->bkhd', k_lat, wk_up)
        v = jnp.einsum('bkhl,ld->bkhd', v_lat, wv_up)
        scores = jnp.einsum('bqhrd,bkhd->bhrqk', q, k) * scale
        causal = jnp.tril(jnp.ones((Tq, Tq), dtype=bool))
        scores = jnp.where(causal, scores, jnp.finfo(scores.dtype).min)
        probs = jax.nn.softmax(scores, axis=-1)
        y = jnp.einsum('bhrqk,bkhd->bqhrd', probs, v)
        y = y.reshape(Bq, Tq, N_HEADS * HEAD_DIM)
        return y @ wo

    def _L0_ffn_ref(tokens, router_w, router_b, expert_weights):
        import jax, jax.numpy as jnp
        import numpy as np
        TOP_K = 2
        EPS = 1e-10
        B, S, H = tokens.shape
        E = expert_weights.shape[0]
        logits = jnp.einsum('bsh,eh->bse', tokens, router_w) + router_b
        probs = jax.nn.softmax(logits, axis=-1)
        top_p, top_i = jax.lax.top_k(probs, TOP_K)
        w = top_p / (jnp.sum(top_p, axis=-1, keepdims=True) + EPS)
        x = tokens.reshape(-1, H)
        idx = top_i.reshape(-1, TOP_K)
        wf = w.reshape(-1, TOP_K)
        y_all = jnp.einsum('nh,ehd->ned', x, expert_weights)
        y_k = jnp.take_along_axis(y_all, idx[:, :, None], axis=1)
        out = jnp.einsum('nk,nkh->nh', wf, y_k)
        acc = jnp.clip(jnp.sum(wf, axis=-1), EPS, None)
        out = (out / acc[:, None]).reshape(B, S, H)
        scale = 1.0 + jnp.sum(w, axis=-1, keepdims=True) * EPS
        return out * scale
    x = L0_attn_x
    x = x + 0.5 * _L0_ffn_ref(_layernorm(x, axis=-1), L0_ffn_router_w, L0_ffn_router_b, L0_ffn_expert_weights)
    x = x + _L0_attn_ref(_layernorm(x, axis=-1), L0_attn_wq, L0_attn_wk_down, L0_attn_wv_down, L0_attn_wk_up, L0_attn_wv_up, L0_attn_wo)
    x = x + 0.5 * _L0_ffn_ref(_layernorm(x, axis=-1), L0_ffn_router_w, L0_ffn_router_b, L0_ffn_expert_weights)
    return x

_drawn_inputs = setup_inputs


def setup_inputs(seed=0):
    import zlib

    import numpy as np

    out = dict(_drawn_inputs(seed))
    spreads = {}
    factors = {}
    for name, (base, spread) in spreads.items():
        noise = np.random.default_rng([zlib.crc32(name.encode()), seed]).standard_normal(out[name].shape)
        drawn = base * np.exp(spread * noise) if base else spread * noise
        out[name] = jnp.asarray(drawn.astype(out[name].dtype))
    for name, factor in factors.items():
        out[name] = (out[name] * factor).astype(out[name].dtype)
    return out
```

```python
from contextlib import ExitStack

import concourse.bass as bass
from concourse import mybir

F32 = mybir.dt.float32
F32R = mybir.dt.float32r
BF16 = mybir.dt.bfloat16
FP16 = mybir.dt.float16
ALU = mybir.AluOpType
ACT = mybir.ActivationFunctionType
AX = mybir.AxisListType

NB, T, D = 4, 1024, 128
P = 128
NT = T // P
CH = 512
NC = T // CH
TC = CH // P
NE = 8
NH, NKV, DL = 8, 2, 32
NR = NH // NKV
SCALE = float(D) ** -0.5
LN_EPS = 1e-5
EPS = 1e-10
MASKED = -1e30

KROWS = 3 * DL + 2
MROW = 3 * DL
VCOLS = 3 * DL + 1
OC = DL + 1

BLOCKS = [(c, j) for c in range(NC) for j in range(TC * (c + 1))]
MBLOCKS = [(i, k) for i in range(NT) for k in range(i // TC + 1)]
NBL = len(BLOCKS)
NS = NH * NBL
MAX_LEAD = 20
ROW_AT = 7
PV_LAG = 3
OUT_LAG = 3
NP = 6
NST = 3

STAT_STEPS = NT + 7
GATE_STEPS = 25
N_DMA = 16


def last_block(u):
    h, c = divmod(u, NC)
    return h * NBL + (TC - 1 if c == 0 else NBL - 1)


def unit_of(s):
    return (s // NBL) * NC + BLOCKS[s % NBL][0]


def offset(s):
    c, j = BLOCKS[s % NBL]
    return max(0, j - TC * c) * P


def on_pool(s):
    return s % 8 != 7


def split_before(s, pool):
    return sum(on_pool(i) == pool for i in range(s + 1))


def macaron(nc, x, wq, wk_down, wv_down, wk_up, wv_up, wo, router_w, router_b, experts, out):
    ctx = ExitStack()
    with ctx:
        def sb(name, shape, dt=F32):
            return ctx.enter_context(nc.sbuf_tensor(name, shape, dt))

        def sem(name):
            return ctx.enter_context(nc.semaphore(name))

        bank = [ctx.enter_context(nc.psum_tensor(f"bank{i}", [P, CH], F32)) for i in range(8)]

        ident = sb("ident", [P, P])
        ident_b = sb("ident_b", [P, P], BF16)
        mask_qk = sb("mask_qk", [P, P], BF16)
        mask_kq = sb("mask_kq", [P, P], BF16)
        fold = sb("fold", [VCOLS, OC])
        rank = sb("rank", [P, NE])
        half_power = sb("half_power", [P, NT])
        wq_sb = sb("wq_sb", [P, NH, D])
        wk_up_sb = sb("wk_up_sb", [DL, D])
        wv_up_sb = sb("wv_up_sb", [DL, D])
        wo_sb = sb("wo_sb", [P, NH, D])
        down_sb = sb("down_sb", [P, 2 * NKV * DL])
        rw_sb = sb("rw_sb", [NE, D])
        rb_sb = sb("rb_sb", [P, NE])
        we_sb = sb("we_sb", [P, NE * D])
        wqT = sb("wqT", [P, NH * D])
        upT = sb("upT", [P, 2 * DL])
        aq_hi = sb("aq_hi", [P, NH * DL], F32R)
        aq_lo = sb("aq_lo", [P, NH * DL], F32R)
        down_hi = sb("down_hi", [P, 2 * NKV * DL], F32R)
        down_lo = sb("down_lo", [P, 2 * NKV * DL], F32R)
        we_hi = sb("we_hi", [P, NE * D], F32R)
        we_lo = sb("we_lo", [P, NE * D], F32R)
        rw_hi = sb("rw_hi", [P, NE], F32R)
        rw_lo = sb("rw_lo", [P, NE], F32R)
        wo_lat = sb("wo_lat", [P, NKV, D])
        x_sb = sb("x_sb", [P, NB * NT, D])
        x1 = sb("x1", [P, NT, D])
        x2 = sb("x2", [P, NT, D])
        x3 = sb("x3", [P, NT, D])
        stats = sb("stats", [P, NT, 6])
        mean = sb("mean", [P, NT])
        diff = sb("diff", [P, NT])
        var_eps = sb("var_eps", [P, NT])
        rstd = sb("rstd", [P, NT])
        xn = sb("xn", [P, NT, D])
        xT_hi = sb("xT_hi", [P, T], F32R)
        xT_lo = sb("xT_lo", [P, T], F32R)
        g_l = sb("g_l", [P, NT, NE])
        g_s = sb("g_s", [P, NT, NE])
        g_e = sb("g_e", [P, NT, NE])
        g_k = sb("g_k", [P, NT, NE])
        g_1 = sb("g_1", [P, NT, NE])
        g_2 = sb("g_2", [P, NT, NE])
        g_r = sb("g_r", [P, 8, NT])
        gate = sb("gate", [P, NT, NE])
        q_hi = sb("q_hi", [P, NKV, T], F32R)
        q_lo = sb("q_lo", [P, NKV, T], F32R)
        k_hi = sb("k_hi", [NKV * DL, T], F32R)
        k_lo = sb("k_lo", [NKV * DL, T], F32R)
        q_stack = sb("q_stack", [KROWS, NH, T], F32R)
        k_stack = sb("k_stack", [KROWS, NKV, T], F32R)
        v_parts = sb("v_parts", [P, NT, NKV, VCOLS + 1], BF16)
        v_rest = sb("v_rest", [P, NT, NKV, DL])
        m_part = sb("m_part", [P, NH, 2, NT])
        m_fin = sb("m_fin", [P, NH, NT])
        mT_hi = sb("mT_hi", [NT, NH, P], F32R)
        mT_lo = sb("mT_lo", [NT, NH, P], F32R)
        prob = sb("prob", [P, NP, CH])
        prob_lo = sb("prob_lo", [P, NP, CH], FP16)
        o_sb = sb("o_sb", [VCOLS, 2, CH])
        rden = sb("rden", [P, 2, TC])
        y_lat = sb("y_lat", [P, NT, NH, DL])
        yT = sb("yT", [P, NKV, T])

        x_loaded = [sem(f"x_loaded{b}") for b in range(NB)]
        w_loaded = sem("w_loaded")
        const_step = sem("const_step")
        ones_set = sem("ones_set")
        prep_pe = sem("prep_pe")
        prep_act = sem("prep_act")
        prep_dve = sem("prep_dve")
        stat_step = sem("stat_step")
        rstd_step = sem("rstd_step")
        xn_ready = sem("xn_ready")
        xT_psum = sem("xT_psum")
        xhi_ready = sem("xhi_ready")
        xlo_ready = sem("xlo_ready")
        logits_done = sem("logits_done")
        gate_step = sem("gate_step")
        gate_exp = sem("gate_exp")
        gate_fin = sem("gate_fin")
        y_done = sem("y_done")
        comb_step = sem("comb_step")
        stored = sem("stored")
        q_done = sem("q_done")
        k_done = sem("k_done")
        v_done = sem("v_done")
        qhi_ready = sem("qhi_ready")
        qlo_ready = sem("qlo_ready")
        khi_ready = sem("khi_ready")
        klo_ready = sem("klo_ready")
        v_step = sem("v_step")
        stacked = sem("stacked")
        mx_done = sem("mx_done")
        mx_red = sem("mx_red")
        m_merged = sem("m_merged")
        mT_psum = sem("mT_psum")
        mhi_ready = sem("mhi_ready")
        mlo_ready = sem("mlo_ready")
        m_row = [sem("m_row0"), sem("m_row1")]
        st_done = sem("st_done")
        p_ready = sem("p_ready")
        split_pool = sem("split_pool")
        split_dve = sem("split_dve")
        pv_done = sem("pv_done")
        o_ready = sem("o_ready")
        ot_done = sem("ot_done")
        norm_step = sem("norm_step")
        yT_psum = sem("yT_psum")
        yT_ready = sem("yT_ready")
        attn_done = sem("attn_done")
        x2_ready = sem("x2_ready")

        N_STACK = N_DMA * 3 * (NH + NKV)
        COMB = NT * NE
        LAYER = {0: 0, 1: 2}

        def bc_e(ap):
            return ap.unsqueeze(2).to_broadcast([P, NT, NE])

        def upper_half(s, w):
            return prob[:, s % NP, :].bitcast(BF16)[:, 1:2 * w:2]

        block = ctx.enter_context(nc.Block())

        @block.sync
        def _(sp):
            sp.dma_start(wq_sb[:], wq.rearrange("m (h d) -> m h d", h=NH)).then_inc(w_loaded, N_DMA)
            sp.dma_start(wk_up_sb[:], wk_up).then_inc(w_loaded, N_DMA)
            sp.dma_start(wv_up_sb[:], wv_up).then_inc(w_loaded, N_DMA)
            sp.dma_start(rw_sb[:], router_w).then_inc(w_loaded, N_DMA)
            sp.dma_start(we_sb[:].rearrange("h (e d) -> h e d", e=NE),
                         experts.rearrange("e h d -> h e d")).then_inc(w_loaded, N_DMA)
            sp.dma_start(wo_sb[:], wo.rearrange("(h d) n -> d h n", h=NH)).then_inc(w_loaded, N_DMA)
            sp.dma_start(down_sb[:, 0:NKV * DL], wk_down).then_inc(w_loaded, N_DMA)
            sp.dma_start(down_sb[:, NKV * DL:], wv_down).then_inc(w_loaded, N_DMA)
            sp.dma_start(rb_sb[:], router_b.unsqueeze(0).to_broadcast([P, NE])).then_inc(w_loaded, N_DMA)
            with sp.Fori(0, NB) as b:
                sp.wait_ge(st_done, b * NS)
                sp.wait_ge(mx_done, b * NS)
                sp.wait_ge(klo_ready, b * NC + NC)
                for g in range(NKV):
                    rows = slice(g * DL, (g + 1) * DL)
                    for n, part in enumerate((k_hi, k_hi, k_lo)):
                        sp.dma_start(k_stack[n * DL:(n + 1) * DL, g, :].bitcast(F32), part[rows, :].bitcast(F32)).then_inc(stacked, N_DMA)
                sp.wait_ge(qlo_ready, b * NKV * NC + NKV * NC)
                for g in range(NKV):
                    for r in range(NR):
                        rows = slice(r * DL, (r + 1) * DL)
                        for n, part in enumerate((q_hi, q_lo, q_hi)):
                            sp.dma_start(q_stack[n * DL:(n + 1) * DL, g * NR + r, :].bitcast(F32),
                                         part[rows, g, :].bitcast(F32)).then_inc(stacked, N_DMA)
                for h in range(NH):
                    sp.wait_ge(mlo_ready, b * NH + h + 1)
                    for n, part in enumerate((mT_hi, mT_lo)):
                        row = q_stack[MROW + n:MROW + n + 1, h, :]
                        sp.dma_start(row.bitcast(F32), part[:, h, :].bitcast(F32)).then_inc(m_row[h % 2], N_DMA)
                sp.wait_ge(comb_step, (b * 2 + 2) * COMB)
                sp.dma_start(out[bass.ds(b, 1)].rearrange("o (t p) d -> p (o t) d", p=P), x3[:]).then_inc(stored, N_DMA)
            sp.wait_ge(stored, NB * N_DMA)

        @block.gpsimd
        def _(pool):
            steps = [0]

            def step(ins):
                ins.then_inc(const_step, 1)
                steps[0] += 1
                pool.wait_ge(const_step, steps[0])

            def select(out, base, pattern, cm, op=ALU.not_equal, fill=1.0):
                step(nc.gpsimd.affine_select(out=out, in_=out, compare_op=op, fill=fill, base=base,
                                             pattern=pattern, channel_multiplier=cm))

            step(nc.gpsimd.memset(ident[:], 0.0))
            select(ident[:], 0, [[-1, P]], 1)
            step(nc.gpsimd.memset(half_power[:], -0.5))
            step(nc.gpsimd.memset(ident_b[:], 0.0))
            select(ident_b[:], 0, [[-1, P]], 1)
            step(nc.gpsimd.memset(mask_qk[:], 0.0))
            select(mask_qk[:], 0, [[-1, P]], 1, ALU.is_ge, MASKED)
            step(nc.gpsimd.memset(mask_kq[:], 0.0))
            select(mask_kq[:], 0, [[1, P]], -1, ALU.is_ge, MASKED)
            step(nc.gpsimd.memset(fold[:], 0.0))
            for n in range(3):
                select(fold[:, 0:DL], -n * DL, [[-1, DL]], 1)
            select(fold[:, DL:OC], -3 * DL, [[0, 1]], 1)
            assert steps[0] == CONST_STEPS

            def norm_power(b, l):
                n = b * 3 + l
                pool.wait_ge(stat_step, (n + 1) * STAT_STEPS)
                pool.wait_ge(xn_ready, n * NT)
                nc.gpsimd.tensor_tensor(rstd[:], var_eps[:], half_power[:], ALU.pow).then_inc(rstd_step, 1)

            def split(b, s):
                w = CH - offset(s)
                pool.wait_ge(p_ready, b * NS + s + 1)
                nc.gpsimd.tensor_tensor(prob_lo[:, s % NP, 0:w], prob[:, s % NP, 0:w],
                                        upper_half(s, w), ALU.subtract).then_inc(split_pool, 1)

            with pool.Fori(0, NB) as b:
                norm_power(b, 0)
                norm_power(b, 1)
                for s in range(NS):
                    if on_pool(s):
                        split(b, s)
                norm_power(b, 2)

        @block.scalar
        def _(act):
            for b in range(NB):
                act.dma_start(x_sb[:, b * NT:(b + 1) * NT, :],
                              x[b].rearrange("(t p) d -> p t d", p=P)).then_inc(x_loaded[b], N_DMA)

            def copy(dst, src):
                return nc.scalar.activation(dst, src, ACT.Copy)

            act.wait_ge(w_loaded, 9 * N_DMA)
            copy(we_hi[:], we_sb[:]).then_inc(prep_act, 1)
            copy(down_hi[:], down_sb[:]).then_inc(prep_act, 1)
            act.wait_ge(prep_pe, 1)
            copy(upT[:], bank[0][:, 0:2 * DL]).then_inc(prep_act, 1)
            copy(rw_hi[:], bank[0][:, 2 * DL:2 * DL + NE]).then_inc(prep_act, 1)
            for n in range(2):
                act.wait_ge(prep_pe, 2 + n)
                copy(wqT[:, n * CH:(n + 1) * CH], bank[1 + n][:]).then_inc(prep_act, 1)
            act.wait_ge(prep_pe, 4)
            copy(aq_hi[:], bank[3][:, 0:NH * DL]).then_inc(prep_act, 1)
            act.wait_ge(prep_pe, 5)
            copy(wo_lat[:].rearrange("p g n -> p (g n)"), bank[4][:, 0:NKV * D]).then_inc(prep_act, 1)

            def high_part(b, l):
                for c in range(NC):
                    n = (b * 3 + l) * NC + c
                    act.wait_ge(xT_psum, n + 1)
                    if l == 0:
                        act.wait_ge(y_done, b * 2 * NT * 2)
                    elif l == 1:
                        act.wait_ge(y_done, b * 2 * NT * 2 + NT * 2)
                    else:
                        act.wait_ge(v_done, b + 1)
                    copy(xT_hi[:, c * CH:(c + 1) * CH], bank[c][:]).then_inc(xhi_ready, 1)

            def gate_exponent(b, f):
                act.wait_ge(gate_step, (b * 2 + f) * GATE_STEPS + 3)
                nc.scalar.activation(g_e[:], g_s[:], ACT.Exp).then_inc(gate_exp, 1)

            def attention(b):
                act.wait_ge(stacked, b * N_STACK)
                for c in range(NC):
                    act.wait_ge(k_done, b * NC + c + 1)
                    copy(k_hi[:, c * CH:(c + 1) * CH], bank[2 + c][0:NKV * DL, :]).then_inc(khi_ready, 1)
                for g in range(NKV):
                    for c in range(NC):
                        act.wait_ge(q_done, b * NKV * NC + g * NC + c + 1)
                        copy(q_hi[:, g, c * CH:(c + 1) * CH], bank[4 + g * NC + c][:]).then_inc(qhi_ready, 1)
                for s in range(-MAX_LEAD, NS + PV_LAG + OUT_LAG):
                    h = (s + ROW_AT) // NBL
                    if (s + ROW_AT) % NBL == 0 and 0 <= h < NH:
                        act.wait_ge(mT_psum, b * NH + h + 1)
                        copy(mT_hi[:, h, :], bank[7][0:NT, 0:P]).then_inc(mhi_ready, 1)
                    if 0 <= s < NS:
                        w = CH - offset(s)
                        act.wait_ge(st_done, b * NS + s + 1)
                        if s >= NP:
                            act.wait_ge(pv_done, b * NS + s - NP + 1)
                        nc.scalar.activation(prob[:, s % NP, 0:w], bank[2 + s % NST][:, 0:w], ACT.Exp,
                                             scale=SCALE).then_inc(p_ready, 1)
                    for u in range(NH * NC):
                        if s == last_block(u) + PV_LAG:
                            act.wait_ge(pv_done, b * NS + last_block(u) + 1)
                            if u >= 2:
                                act.wait_ge(ot_done, b * NH * NC + u - 1)
                            copy(o_sb[:, u % 2, :], bank[5 + u % 2][0:VCOLS, :]).then_inc(o_ready, 1)
                for n in range(NKV * NC):
                    act.wait_ge(yT_psum, b * NKV * NC + n + 1)
                    g, c = divmod(n, NC)
                    copy(yT[:, g, c * CH:(c + 1) * CH], bank[n][:]).then_inc(yT_ready, 1)

            with act.Fori(0, NB) as b:
                high_part(b, 0)
                gate_exponent(b, 0)
                high_part(b, 1)
                attention(b)
                high_part(b, 2)
                gate_exponent(b, 1)

        @block.vector
        def _(dve):
            for e in range(NE):
                nc.vector.memset(rank[:, e:e + 1], float(NE - e)).then_inc(ones_set, 1)
            nc.vector.memset(m_part[:], -3e38).then_inc(ones_set, 1)
            nc.vector.memset(v_parts[:, :, :, VCOLS - 1:VCOLS], 1.0).then_inc(ones_set, 1)
            nc.vector.memset(k_stack[MROW:KROWS, :, :].bitcast(F32), -1.0).then_inc(ones_set, 1)

            def low(dst, src, hi):
                return nc.vector.tensor_tensor(dst, src, hi.bitcast(F32), ALU.subtract)

            dve.wait_ge(prep_act, 1)
            low(we_lo[:], we_sb[:], we_hi[:]).then_inc(prep_dve, 1)
            dve.wait_ge(prep_act, 2)
            low(down_lo[:], down_sb[:], down_hi[:]).then_inc(prep_dve, 1)
            dve.wait_ge(prep_act, 4)
            low(rw_lo[:], bank[0][:, 2 * DL:2 * DL + NE], rw_hi[:]).then_inc(prep_dve, 1)
            dve.wait_ge(prep_act, 7)
            low(aq_lo[:], bank[3][:, 0:NH * DL], aq_hi[:]).then_inc(prep_dve, 1)

            def layer_norm(b, l, src):
                n = b * 3 + l
                for t in range(NT):
                    nc.vector.bn_stats(stats[:, t, :], src(t)).then_inc(stat_step, 1)
                k = [NT]

                def step(ins):
                    ins.then_inc(stat_step, 1)
                    k[0] += 1
                    dve.wait_ge(stat_step, n * STAT_STEPS + k[0])

                V = nc.vector
                mean_e, sq_e, mean_o, sq_o = (stats[:, :, i] for i in (1, 2, 4, 5))
                dve.wait_ge(stat_step, n * STAT_STEPS + NT)
                step(V.tensor_tensor(mean[:], mean_e, mean_o, ALU.add))
                step(V.tensor_tensor(diff[:], mean_e, mean_o, ALU.subtract))
                step(V.tensor_tensor(diff[:], diff[:], diff[:], ALU.mult))
                step(V.tensor_tensor(var_eps[:], sq_e, sq_o, ALU.add))
                step(V.tensor_scalar(diff[:], diff[:], 0.25, LN_EPS, ALU.mult, ALU.add))
                step(V.scalar_tensor_tensor(out=var_eps[:], in0=var_eps[:], scalar=1.0 / D, in1=diff[:],
                                            op0=ALU.mult, op1=ALU.add))
                step(V.tensor_scalar(mean[:], mean[:], 0.5, None, ALU.mult))
                assert k[0] == STAT_STEPS
                dve.wait_ge(rstd_step, n + 1)
                dve.wait_ge(xT_psum, n * NC)
                for t in range(NT):
                    nc.vector.tensor_scalar(xn[:, t, :], src(t), mean[:, t:t + 1], rstd[:, t:t + 1],
                                            ALU.subtract, ALU.mult).then_inc(xn_ready, 1)
                for c in range(NC):
                    dve.wait_ge(xhi_ready, n * NC + c + 1)
                    low(xT_lo[:, c * CH:(c + 1) * CH], bank[c][:], xT_hi[:, c * CH:(c + 1) * CH])\
                        .then_inc(xlo_ready, 1)

            def routing(b, f):
                base = (b * 2 + f) * GATE_STEPS
                k = [0]

                def step(ins):
                    ins.then_inc(gate_step, 1)
                    k[0] += 1
                    dve.wait_ge(gate_step, base + k[0])

                V = nc.vector
                r = [g_r[:, i, :] for i in range(8)]
                dve.wait_ge(logits_done, b * 2 + f + 1)
                logits = bank[2][:, 0:NT * NE].rearrange("p (t e) -> p t e", t=NT)
                step(V.tensor_tensor(g_l[:], logits, rb_sb[:].unsqueeze(1).to_broadcast([P, NT, NE]), ALU.add))
                step(V.reduce_max(r[0], g_l[:], AX.X))
                step(V.tensor_tensor(g_s[:], g_l[:], bc_e(r[0]), ALU.subtract))
                rank_b = rank[:].unsqueeze(1).to_broadcast([P, NT, NE])
                step(V.scalar_tensor_tensor(out=g_k[:], in0=g_s[:], scalar=0.0, in1=rank_b,
                                            op0=ALU.is_ge, op1=ALU.mult))
                step(V.reduce_max(r[1], g_k[:], AX.X))
                step(V.tensor_tensor(g_1[:], g_k[:], bc_e(r[1]), ALU.is_equal))
                step(V.scalar_tensor_tensor(out=g_2[:], in0=g_1[:], scalar=-3e38, in1=g_s[:],
                                            op0=ALU.mult, op1=ALU.add))
                step(V.reduce_max(r[2], g_2[:], AX.X))
                step(V.tensor_tensor(g_k[:], g_2[:], bc_e(r[2]), ALU.is_ge))
                step(V.tensor_tensor(g_k[:], g_k[:], rank_b, ALU.mult))
                step(V.reduce_max(r[3], g_k[:], AX.X))
                step(V.tensor_tensor(g_2[:], g_k[:], bc_e(r[3]), ALU.is_equal))
                step(V.tensor_tensor(g_1[:], g_1[:], g_2[:], ALU.add))
                dve.wait_ge(gate_exp, b * 2 + f + 1)
                step(V.reduce_sum(r[4], g_e[:], AX.X))
                step(V.reciprocal(r[4], r[4]))
                step(V.tensor_tensor(g_l[:], g_e[:], bc_e(r[4]), ALU.mult))
                step(V.tensor_tensor(g_l[:], g_l[:], g_1[:], ALU.mult))
                step(V.reduce_sum(r[5], g_l[:], AX.X))
                step(V.tensor_scalar(r[5], r[5], EPS, None, ALU.add))
                step(V.reciprocal(r[5], r[5]))
                step(V.tensor_tensor(g_l[:], g_l[:], bc_e(r[5]), ALU.mult))
                step(V.reduce_sum(r[6], g_l[:], AX.X))
                step(V.tensor_scalar(r[7], r[6], EPS, 1.0, ALU.mult, ALU.add))
                step(V.tensor_scalar(r[6], r[6], EPS, 2.0, ALU.max, ALU.mult))
                step(V.reciprocal(r[6], r[6]))
                assert k[0] == GATE_STEPS
                V.tensor_tensor(r[7], r[7], r[6], ALU.mult).then_inc(gate_fin, 1)
                dve.wait_ge(gate_fin, (b * 2 + f) * 2 + 1)
                V.tensor_tensor(gate[:], g_l[:], bc_e(r[7]), ALU.mult).then_inc(gate_fin, 1)

            def combine(b, f, src, dst):
                base = (b * 2 + f) * COMB
                jobs = (b * 2 + f) * 2 * NT
                dve.wait_ge(gate_fin, (b * 2 + f) * 2 + 2)
                if f == 1:
                    dve.wait_ge(stored, b * N_DMA)
                for p in range(NT // 2):
                    for half in range(2):
                        for e in range(NE // 2):
                            for tt in range(2):
                                t, ee = 2 * p + tt, half * NE // 2 + e
                                n = 4 * p + 2 * half + tt
                                i = 16 * p + 8 * half + 2 * e + tt
                                if e == 0:
                                    dve.wait_ge(y_done, jobs + n + 1)
                                if ee:
                                    dve.wait_ge(comb_step, base + i - 1)
                                nc.vector.scalar_tensor_tensor(
                                    out=dst[:, t, :], in0=bank[4 + n % 4][:, e * D:(e + 1) * D],
                                    scalar=gate[:, t, ee:ee + 1], in1=dst[:, t, :] if ee else src(t),
                                    op0=ALU.mult, op1=ALU.add).then_inc(comb_step, 1)
                dve.wait_ge(comb_step, base + COMB)

            def split(b, s):
                w = CH - offset(s)
                dve.wait_ge(p_ready, b * NS + s + 1)
                nc.vector.tensor_tensor(prob_lo[:, s % NP, 0:w], prob[:, s % NP, 0:w],
                                        upper_half(s, w), ALU.subtract).then_inc(split_dve, 1)

            def attention(b):
                for c in range(NC):
                    cols = slice(c * CH, (c + 1) * CH)
                    dve.wait_ge(khi_ready, b * NC + c + 1)
                    low(k_lo[:, cols], bank[2 + c][0:NKV * DL, :], k_hi[:, cols]).then_inc(klo_ready, 1)
                for g in range(NKV):
                    for c in range(NC):
                        cols = slice(c * CH, (c + 1) * CH)
                        dve.wait_ge(qhi_ready, b * NKV * NC + g * NC + c + 1)
                        low(q_lo[:, g, cols], bank[4 + g * NC + c][:], q_hi[:, g, cols]).then_inc(qlo_ready, 1)
                v_psum = bank[0][:].rearrange("p (t g l) -> p t g l", t=NT, g=NKV)
                part = [v_parts[:, :, :, n * DL:(n + 1) * DL] for n in range(3)]
                dve.wait_ge(v_done, b + 1)
                dve.wait_ge(pv_done, b * NS)
                nc.vector.tensor_copy(part[0], v_psum).then_inc(v_step, 1)
                dve.wait_ge(v_step, b * 4 + 1)
                nc.vector.tensor_tensor(v_rest[:], v_psum, part[0], ALU.subtract).then_inc(v_step, 1)
                dve.wait_ge(v_step, b * 4 + 2)
                nc.vector.tensor_copy(part[1], v_rest[:]).then_inc(v_step, 1)
                dve.wait_ge(v_step, b * 4 + 3)
                nc.vector.tensor_tensor(part[2], v_rest[:], part[1], ALU.subtract).then_inc(v_step, 1)

                for s in range(-MAX_LEAD, NS + PV_LAG + OUT_LAG + 1):
                    h = (s + ROW_AT) // NBL
                    if (s + ROW_AT) % NBL == 0 and 0 <= h < NH:
                        dve.wait_ge(mhi_ready, b * NH + h + 1)
                        low(mT_lo[:, h, :], bank[7][0:NT, 0:P], mT_hi[:, h, :]).then_inc(mlo_ready, 1)
                    m = s + MAX_LEAD
                    if m < NS:
                        hm, (i, k) = m // NBL, MBLOCKS[m % NBL]
                        w = min(CH, (i + 1) * P - k * CH)
                        dve.wait_ge(mx_done, b * NS + m + 1)
                        nc.vector.reduce_max(m_part[:, hm, k, i:i + 1], bank[m % 2][:, 0:w], AX.X)\
                            .then_inc(mx_red, 1)
                        if m % NBL == NBL - 1:
                            dve.wait_ge(mx_red, b * NS + m + 1)
                            nc.vector.tensor_tensor(m_fin[:, hm, :], m_part[:, hm, 0, :], m_part[:, hm, 1, :],
                                                    ALU.max).then_inc(m_merged, 1)
                    if 0 <= s < NS and not on_pool(s):
                        split(b, s)
                    for u in range(NH * NC):
                        if s == last_block(u) + PV_LAG + OUT_LAG + 1:
                            h, c = divmod(u, NC)
                            dve.wait_ge(ot_done, b * NH * NC + u + 1)
                            oT = bank[7][:, P:P + TC * OC].rearrange("p (t v) -> p t v", t=TC)
                            nc.vector.reciprocal(rden[:, u % 2, :], oT[:, :, DL]).then_inc(norm_step, 1)
                            dve.wait_ge(norm_step, b * 2 * NH * NC + 2 * u + 1)
                            nc.vector.tensor_tensor(
                                y_lat[:, c * TC:(c + 1) * TC, h, :], oT[:, :, 0:DL],
                                rden[:, u % 2, :].unsqueeze(2).to_broadcast([P, TC, DL]), ALU.mult)\
                                .then_inc(norm_step, 1)
                for c in range(NC):
                    dve.wait_ge(attn_done, b * NC + c + 1)
                    tiles = slice(c * TC, (c + 1) * TC)
                    nc.vector.tensor_tensor(x2[:, tiles, :], bank[5 + c][:].rearrange("p (t d) -> p t d", t=TC),
                                            x1[:, tiles, :], ALU.add).then_inc(x2_ready, 1)
                dve.wait_ge(x2_ready, b * NC + NC)

            dve.wait_ge(ones_set, NE + 3)
            for b in range(NB):
                dve.wait_ge(x_loaded[b], N_DMA)
            with dve.Fori(0, NB) as b:
                def x_tile(t):
                    return x_sb[:, bass.ds(b * NT + t, 1), :].rearrange("p o d -> p (o d)")

                layer_norm(b, 0, x_tile)
                routing(b, 0)
                combine(b, 0, x_tile, x1)
                layer_norm(b, 1, lambda t: x1[:, t, :])
                attention(b)
                layer_norm(b, 2, lambda t: x2[:, t, :])
                routing(b, 1)
                combine(b, 1, lambda t: x2[:, t, :], x3)

        @block.tensor
        def _(pe):
            mm = nc.tensor.matmul

            pe.wait_ge(const_step, CONST_STEPS)
            pe.wait_ge(w_loaded, 9 * N_DMA)
            nc.tensor.transpose(bank[0][:, 0:DL], wk_up_sb[:], ident[0:DL, 0:DL])
            nc.tensor.transpose(bank[0][:, DL:2 * DL], wv_up_sb[:], ident[0:DL, 0:DL])
            nc.tensor.transpose(bank[0][:, 2 * DL:2 * DL + NE], rw_sb[:], ident[0:NE, 0:NE]).then_inc(prep_pe, 1)
            for n in range(2):
                for i in range(NH // 2):
                    last = nc.tensor.transpose(bank[1 + n][:, i * P:(i + 1) * P], wq_sb[:, n * NH // 2 + i, :],
                                               ident[:])
                last.then_inc(prep_pe, 1)
            pe.wait_ge(prep_act, 6)
            for h in range(NH):
                last = mm(bank[3][:, h * DL:(h + 1) * DL], wqT[:, h * D:(h + 1) * D], upT[:, 0:DL],
                          start=True, stop=True)
            last.then_inc(prep_pe, 1)
            for h in range(NH):
                g, r = divmod(h, NR)
                last = mm(bank[4][r * DL:(r + 1) * DL, g * D:(g + 1) * D], upT[:, DL:2 * DL], wo_sb[:, h, :],
                          start=True, stop=True)
            last.then_inc(prep_pe, 1)
            pe.wait_ge(prep_act, 8)
            pe.wait_ge(prep_dve, 4)

            def transposes(b, l):
                n = b * 3 + l
                pe.wait_ge(xlo_ready, n * NC)
                if l == 2:
                    pe.wait_ge(yT_ready, b * NKV * NC + NKV * NC)
                for c in range(NC):
                    for i in range(TC):
                        pe.wait_ge(xn_ready, n * NT + c * TC + i + 1)
                        last = nc.tensor.transpose(bank[c][:, i * P:(i + 1) * P], xn[:, c * TC + i, :], ident[:])
                    last.then_inc(xT_psum, 1)

            def three(dst, lhs, rhs):
                mm(dst, lhs[0], rhs[0], start=True, stop=False)
                mm(dst, lhs[0], rhs[1], start=False, stop=False)
                return mm(dst, lhs[1], rhs[0], start=False, stop=True)

            def both(hi, lo, *at):
                return hi[at], lo[at]

            def x_part(t):
                return both(xT_hi, xT_lo, slice(None), slice(t * P, (t + 1) * P))

            def expert_layer(b, f):
                n = b * 2 + f
                pe.wait_ge(xlo_ready, (b * 3 + LAYER[f]) * NC + NC)
                pe.wait_ge(gate_step, n * GATE_STEPS)
                for t in range(NT):
                    last = three(bank[2][:, t * NE:(t + 1) * NE], x_part(t), (rw_hi[:], rw_lo[:]))
                last.then_inc(logits_done, 1)
                for p in range(NT // 2):
                    for half in range(2):
                        for tt in range(2):
                            j = 4 * p + 2 * half + tt
                            used = n * COMB + (16 * (p - 1) + 8 * half + 7 + tt if p else 0)
                            pe.wait_ge(comb_step, used)
                            three(bank[4 + j % 4][:], x_part(2 * p + tt),
                                  both(we_hi, we_lo, slice(None), slice(half * CH, (half + 1) * CH)))\
                                .then_inc(y_done, 1)

            def attention(b):
                pe.wait_ge(xlo_ready, (b * 3 + 1) * NC + NC)
                nk = NKV * DL
                for c in range(NC):
                    three(bank[2 + c][0:nk, :], (down_hi[:, 0:nk], down_lo[:, 0:nk]),
                          both(xT_hi, xT_lo, slice(None), slice(c * CH, (c + 1) * CH))).then_inc(k_done, 1)
                for g in range(NKV):
                    for c in range(NC):
                        three(bank[4 + g * NC + c][:], both(aq_hi, aq_lo, slice(None), slice(g * P, (g + 1) * P)),
                              both(xT_hi, xT_lo, slice(None), slice(c * CH, (c + 1) * CH))).then_inc(q_done, 1)
                for t in range(NT):
                    last = three(bank[0][:, t * nk:(t + 1) * nk], x_part(t), (down_hi[:, nk:], down_lo[:, nk:]))
                last.then_inc(v_done, 1)

                def maximum(m):
                    h, (i, k) = m // NBL, MBLOCKS[m % NBL]
                    w = min(CH, (i + 1) * P - k * CH)
                    diagonal = k == i // TC
                    if m >= 2:
                        pe.wait_ge(mx_red, b * NS + m - 1)
                    elif m == 0:
                        pe.wait_ge(v_step, b * 4 + 2)
                        pe.wait_ge(stacked, b * N_STACK + N_STACK)
                    last = mm(bank[m % 2][:, 0:w], q_stack[0:MROW, h, i * P:(i + 1) * P],
                              k_stack[0:MROW, h // NR, k * CH:k * CH + w], start=True, stop=not diagonal)
                    if diagonal:
                        last = mm(bank[m % 2][:, w - P:w], ident_b[:], mask_qk[:], start=False, stop=True)
                    last.then_inc(mx_done, 1)

                def scores(s):
                    h, (c, j) = s // NBL, BLOCKS[s % NBL]
                    off = offset(s)
                    w = CH - off
                    diagonal = j >= TC * c
                    if s >= NST:
                        pe.wait_ge(p_ready, b * NS + s - NST + 1)
                    elif s == 0:
                        pe.wait_ge(klo_ready, b * NC + NC)
                        pe.wait_ge(qlo_ready, b * NKV * NC + NKV * NC)
                    if s % NBL == 0:
                        pe.wait_ge(m_row[h % 2], (b * NH // 2 + h // 2 + 1) * 2 * N_DMA)
                    last = mm(bank[2 + s % NST][:, 0:w], k_stack[:, h // NR, j * P:(j + 1) * P],
                              q_stack[:, h, c * CH + off:(c + 1) * CH], start=True, stop=not diagonal)
                    if diagonal:
                        last = mm(bank[2 + s % NST][:, 0:P], ident_b[:], mask_kq[:], start=False, stop=True)
                    last.then_inc(st_done, 1)

                def values(s):
                    h, (c, j) = s // NBL, BLOCKS[s % NBL]
                    off = offset(s)
                    w = CH - off
                    u = unit_of(s)
                    first, final = j == 0, s == last_block(u)
                    if s == 0:
                        pe.wait_ge(v_step, b * 4 + 4)
                    mine, n = (split_pool, split_before(s, True)) if on_pool(s) else (split_dve, split_before(s, False))
                    pe.wait_ge(mine, b * split_before(NS - 1, on_pool(s)) + n)
                    if first and u >= 2:
                        pe.wait_ge(o_ready, b * NH * NC + u - 1)
                    acc = bank[5 + u % 2][0:VCOLS, off:CH]
                    v = v_parts[:, j, h // NR, 0:VCOLS]
                    mm(acc, v, upper_half(s, w), start=first, stop=False)
                    mm(acc, v, prob_lo[:, s % NP, 0:w], start=False, stop=final).then_inc(pv_done, 1)

                for s in range(-MAX_LEAD, NS + PV_LAG + OUT_LAG + 1):
                    h = (s + ROW_AT) // NBL
                    if (s + ROW_AT) % NBL == 0 and 0 <= h < NH:
                        pe.wait_ge(m_merged, b * NH + h + 1)
                        pe.wait_ge(mlo_ready, b * NH + h)
                        done = sum(last_block(u) + PV_LAG + OUT_LAG < s for u in range(NH * NC))
                        pe.wait_ge(norm_step, (b * NH * NC + done) * 2)
                        nc.tensor.transpose(bank[7][0:NT, 0:P], m_fin[:, h, :], ident[:]).then_inc(mT_psum, 1)
                    if 0 <= s < NS:
                        scores(s)
                    if s + MAX_LEAD < NS:
                        maximum(s + MAX_LEAD)
                    if 0 <= s - PV_LAG < NS:
                        values(s - PV_LAG)
                    for u in range(NH * NC):
                        if s == last_block(u) + PV_LAG + OUT_LAG:
                            pe.wait_ge(o_ready, b * NH * NC + u + 1)
                            rows = sum(-ROW_AT + hh * NBL <= s for hh in range(NH))
                            pe.wait_ge(mlo_ready, b * NH + rows)
                            pe.wait_ge(norm_step, (b * NH * NC + u) * 2)
                            for i in range(TC):
                                last = mm(bank[7][:, P + i * OC:P + (i + 1) * OC],
                                          o_sb[:, u % 2, i * P:(i + 1) * P], fold[:], start=True, stop=True)
                            last.then_inc(ot_done, 1)
                pe.wait_ge(norm_step, (b + 1) * NH * NC * 2)
                for g in range(NKV):
                    for c in range(NC):
                        for i in range(TC):
                            last = nc.tensor.transpose(bank[g * NC + c][:, i * P:(i + 1) * P],
                                                       y_lat[:, c * TC + i, g * NR:(g + 1) * NR, :]
                                                       .rearrange("p r l -> p (r l)"), ident[:])
                        last.then_inc(yT_psum, 1)
                pe.wait_ge(yT_ready, (b + 1) * NKV * NC)
                for c in range(NC):
                    for i in range(TC):
                        t = c * TC + i
                        for g in range(NKV):
                            last = mm(bank[5 + c][:, i * D:(i + 1) * D], yT[:, g, t * P:(t + 1) * P],
                                      wo_lat[:, g, :], start=g == 0, stop=g == NKV - 1)
                    last.then_inc(attn_done, 1)

            with pe.Fori(0, NB) as b:
                transposes(b, 0)
                expert_layer(b, 0)
                transposes(b, 1)
                attention(b)
                transposes(b, 2)
                expert_layer(b, 1)


CONST_STEPS = 14

_INS = ["L0_attn_x", "L0_attn_wq", "L0_attn_wk_down", "L0_attn_wv_down", "L0_attn_wk_up", "L0_attn_wv_up",
        "L0_attn_wo", "L0_ffn_router_w", "L0_ffn_router_b", "L0_ffn_expert_weights"]


def kernel(**inputs):
    import numpy as np
    import concourse.bacc as bacc
    from concourse.bass_utils import run_bass_kernel_spmd

    nc = bacc.Bacc("TRN2", target_bir_lowering=False, num_devices=1)
    arrays, args = {}, []
    for name in _INS:
        a = np.ascontiguousarray(inputs[name])
        arrays[f"in_{name}"] = a
        args.append(nc.dram_tensor(f"in_{name}", a.shape, mybir.dt.from_np(a.dtype), kind="ExternalInput").ap())
    out = nc.dram_tensor("out_x", (NB, T, D), F32, kind="ExternalOutput").ap()
    macaron(nc, *args, out)
    r = run_bass_kernel_spmd(nc, [arrays], core_ids=[0])
    return np.asarray(r.results[0]["out_x"])
```

```python
from contextlib import ExitStack

import concourse.bass as bass
from concourse import mybir

F32 = mybir.dt.float32
F32R = mybir.dt.float32r
BF16 = mybir.dt.bfloat16
FP16 = mybir.dt.float16
ALU = mybir.AluOpType
ACT = mybir.ActivationFunctionType
AX = mybir.AxisListType

NB, T, D = 4, 1024, 128
P = 128
NT = T // P
CH = 512
NC = T // CH
TC = CH // P
NE = 8
NH, NKV, DL = 8, 2, 32
NR = NH // NKV
NU = NH * NC
SCALE = float(D) ** -0.5
LN_EPS = 1e-5
EPS = 1e-10
MASKED = -1e30

MROW = 3 * DL
KROWS = MROW + 2
VCOLS = 3 * DL + 1

BLOCKS = [(c, j) for c in range(NC) for j in range(TC * (c + 1))]
MBLOCKS = [(i, k) for i in range(NT) for k in range(i // TC + 1)]
NBL = len(BLOCKS)
NS = NH * NBL
GS = NS // NKV

MAX_LEAD = 22
ROW_LEAD = 7
PV_LAG = 4
PV_HOLD = 2
NORM_LAG = PV_LAG + 1
NP = 8
NST = 2

MX, ST, OB, FB = 0, 2, 4, 5
NFB = 3

CUT = 5
JOIN = 5
KEEP = 12
FRONT = 11
BACK = 62
STACK_1, VPARTS_1 = 3, 3 + PV_LAG
POWER, XN, XT, XLO = 4, 5, 6, 7
LOGITS, ROUTE, Y, PICK = 9, 10, 11, 3
ROUTE_SLOTS = 4
LN1 = FRONT + Y + 28
PROJ = LN1 + 9
STACK_0 = PROJ + 7

STAT_STEPS = 7
GATE_STEPS = 25
N_DMA = 16
TILE_STEPS = NE + 1
COMB = NT * TILE_STEPS
JOBS = 2 * NT
CONST_STEPS = 9


def last_block(u):
    h, c = divmod(u, NC)
    return h * NBL + (TC - 1 if c == 0 else NBL - 1)


UNIT_ENDS = {last_block(u): u for u in range(NU)}


def offset(s):
    c, j = BLOCKS[s % NBL]
    return max(0, j - TC * c) * P


def on_pool(s):
    return s % 24 != 23


def values_slot(s):
    n = BLOCKS[s % NBL][1]
    return s + max(0, PV_HOLD - n) + PV_LAG


def job_slot(j):
    return j * 3 // 2


JOB_AT = {job_slot(j): j for j in range(JOBS)}

ENTRIES = []
for _m in range(NS):
    if _m % NBL == MAX_LEAD - NBL - ROW_LEAD:
        ENTRIES.append(("row", _m // NBL - 1))
    ENTRIES.append(("block", _m))
ENTRY = {e: n for n, e in enumerate(ENTRIES)}
assert len(ENTRIES) % 2 == 0


def splits(s, pool):
    return sum(on_pool(i) == pool for i in range(s + 1))


def at(k, s):
    return k + s // NS if s // NS else k, s % NS


def real(b):
    return not isinstance(b, int) or 0 <= b < NB


def need(engine, semaphore, value):
    if not isinstance(value, int) or value > 0:
        engine.wait_ge(semaphore, value)


def timeline(engine, slot, front, join, back):
    for s in range(FRONT, CUT + NS):
        front(0, s)

    def run(k, lo, hi):
        for s in range(lo, hi):
            slot(k, s)
            if s >= CUT:
                if real(k - 1):
                    join(k - 1, s)
                if real(k + 1):
                    front(k + 1, s)
                if real(k - 1):
                    back(k - 1, s)

    run(0, -MAX_LEAD, CUT + NS)
    with engine.Fori(1, NB - 1) as k:
        run(k, CUT, CUT + NS)
    run(NB - 1, CUT, CUT + NS)
    for s in range(CUT, CUT + NS):
        slot(NB, s)
        join(NB - 1, s)
        back(NB - 1, s)


def macaron(nc, x, wq, wk_down, wv_down, wk_up, wv_up, wo, router_w, router_b, experts, out):
    ctx = ExitStack()
    with ctx:
        def sb(name, shape, dt=F32):
            return ctx.enter_context(nc.sbuf_tensor(name, shape, dt))

        def sem(name):
            return ctx.enter_context(nc.semaphore(name))

        def sems(name, n):
            return [sem(f"{name}{i}") for i in range(n)]

        bank = [ctx.enter_context(nc.psum_tensor(f"bank{i}", [P, CH], F32)) for i in range(8)]

        ident = sb("ident", [P, P])
        ident_b = sb("ident_b", [P, P], BF16)
        mask_qk = sb("mask_qk", [P, P], BF16)
        mask_kq = sb("mask_kq", [P, P], BF16)
        rank = sb("rank", [P, NE])
        half_power = sb("half_power", [P, NT])
        wq_sb = sb("wq_sb", [P, NH, D])
        wk_up_sb = sb("wk_up_sb", [DL, D])
        wv_up_sb = sb("wv_up_sb", [DL, D])
        wo_sb = sb("wo_sb", [P, NH, D])
        down_sb = sb("down_sb", [P, 2 * NKV * DL])
        rw_sb = sb("rw_sb", [NE, D])
        rb_sb = sb("rb_sb", [P, NE])
        we_sb = sb("we_sb", [P, NE * D])
        wqT = sb("wqT", [P, NH * D])
        upT = sb("upT", [P, 2 * DL])
        aq_hi = sb("aq_hi", [P, NH * DL], F32R)
        aq_lo = sb("aq_lo", [P, NH * DL], F32R)
        down_hi = sb("down_hi", [P, 2 * NKV * DL], F32R)
        down_lo = sb("down_lo", [P, 2 * NKV * DL], F32R)
        we_hi = sb("we_hi", [P, NE * D], F32R)
        we_lo = sb("we_lo", [P, NE * D], F32R)
        rw_hi = sb("rw_hi", [P, NE], F32R)
        rw_lo = sb("rw_lo", [P, NE], F32R)
        wo_lat = sb("wo_lat", [P, NKV, D])
        x0 = sb("x0", [P, NT, D])
        x1 = sb("x1", [P, NT, D])
        x1_kept = sb("x1_kept", [P, NT, D])
        x2 = sb("x2", [P, NT, D])
        x3 = sb("x3", [P, NT, D])
        stats = sb("stats", [P, NT, 6])
        neg_mean = sb("neg_mean", [P, NT])
        diff = sb("diff", [P, NT])
        var_eps = sb("var_eps", [P, NT])
        rstd = sb("rstd", [P, NT])
        shift = sb("shift", [P, NT])
        xn = sb("xn", [P, NT, D])
        xT_hi = sb("xT_hi", [P, T], F32R)
        xT_lo = sb("xT_lo", [P, T], F32R)
        g_l = sb("g_l", [P, NT, NE])
        g_s = sb("g_s", [P, NT, NE])
        g_e = sb("g_e", [P, NT, NE])
        g_k = sb("g_k", [P, NT, NE])
        g_1 = sb("g_1", [P, NT, NE])
        g_2 = sb("g_2", [P, NT, NE])
        g_r = sb("g_r", [P, 8, NT])
        gate = sb("gate", [P, NT, NE])
        odd_sum = sb("odd_sum", [P, 2, D])
        q_hi = sb("q_hi", [P, NKV, T], F32R)
        q_lo = sb("q_lo", [P, NKV, T], F32R)
        k_hi = sb("k_hi", [NKV * DL, T], F32R)
        k_lo = sb("k_lo", [NKV * DL, T], F32R)
        q_stack = sb("q_stack", [KROWS, NH, T], F32R)
        k_stack = sb("k_stack", [KROWS, NKV, T], F32R)
        v_lat = sb("v_lat", [P, NT, NKV, DL])
        v_parts = sb("v_parts", [P, NT, NKV, VCOLS + 1], BF16)
        v_rest = sb("v_rest", [P, NT, DL])
        m_part = sb("m_part", [P, NH, 2, NT])
        m_fin = sb("m_fin", [P, NH, NT])
        mT = sb("mT", [NT, NH, P])
        mT_hi = sb("mT_hi", [NT, NH, P], F32R)
        mT_lo = sb("mT_lo", [NT, NH, P], F32R)
        prob = sb("prob", [P, NP, CH])
        prob_lo = sb("prob_lo", [P, NP, CH], FP16)
        rden = sb("rden", [P, 2, TC])
        o_sum = sb("o_sum", [P, 2, TC, DL])
        y_lat = sb("y_lat", [P, NT, NH, DL])
        yT = sb("yT", [P, NKV, T])

        w_loaded = sem("w_loaded")
        const_step = sem("const_step")
        set_up = sem("set_up")
        prep_pe = sem("prep_pe")
        prep_act = sem("prep_act")
        prep_dve = sem("prep_dve")
        x_loaded = sem("x_loaded")
        bn_done = sems("bn_done", 3)
        stat_step = sems("stat_step", 3)
        rstd_step = sems("rstd_step", 3)
        xn_ready = sems("xn_ready", 3)
        xT_psum = sems("xT_psum", 3)
        xhi_ready = sems("xhi_ready", 3)
        xlo_ready = sems("xlo_ready", 3)
        logits_done = sems("logits_done", 2)
        gate_step = sems("gate_step", 2)
        gate_exp = sems("gate_exp", 2)
        y_done = sems("y_done", 2)
        comb = sems("comb", 2)
        stored = sem("stored")
        kept = sem("kept")
        q_done = sem("q_done")
        k_done = sem("k_done")
        v_done = sem("v_done")
        qhi_ready = sem("qhi_ready")
        qlo_ready = sem("qlo_ready")
        khi_ready = sem("khi_ready")
        klo_ready = sem("klo_ready")
        v_ready = sem("v_ready")
        v_step = sems("v_step", NKV)
        stacked = sems("stacked", NH)
        mx_done = sem("mx_done")
        mx_red = sem("mx_red")
        m_merged = sem("m_merged")
        mT_psum = sem("mT_psum")
        mT_ready = sem("mT_ready")
        mlo_ready = sem("mlo_ready")
        m_row = sems("m_row", 2)
        st_done = sem("st_done")
        p_ready = sem("p_ready")
        split_done = {True: sem("split_pool"), False: sem("split_dve")}
        pv_done = sem("pv_done")
        norm_step = sem("norm_step")
        yT_psum = sem("yT_psum")
        yT_ready = sem("yT_ready")
        attn_done = sem("attn_done")
        x2_ready = sem("x2_ready")
        CREDIT = 1

        def per_expert(ap):
            return ap.unsqueeze(2).to_broadcast([P, NT, NE])

        def upper_half(s, w):
            return prob[:, s % NP, :].bitcast(BF16)[:, 1:2 * w:2]

        def cols(c):
            return slice(c * CH, (c + 1) * CH)

        block = ctx.enter_context(nc.Block())

        @block.sync
        def _(sp):
            sp.dma_start(wk_up_sb[:], wk_up).then_inc(w_loaded, N_DMA)
            sp.dma_start(wv_up_sb[:], wv_up).then_inc(w_loaded, N_DMA)
            sp.dma_start(rw_sb[:], router_w).then_inc(w_loaded, N_DMA)
            sp.dma_start(rb_sb[:], router_b.unsqueeze(0).to_broadcast([P, NE])).then_inc(w_loaded, N_DMA)
            sp.dma_start(wq_sb[:], wq.rearrange("m (h d) -> m h d", h=NH)).then_inc(w_loaded, N_DMA)
            sp.dma_start(we_sb[:].rearrange("h (e d) -> h e d", e=NE),
                         experts.rearrange("e h d -> h e d")).then_inc(w_loaded, N_DMA)
            sp.dma_start(down_sb[:, 0:NKV * DL], wk_down).then_inc(w_loaded, N_DMA)
            sp.dma_start(down_sb[:, NKV * DL:], wv_down).then_inc(w_loaded, N_DMA)
            sp.dma_start(wo_sb[:], wo.rearrange("(h d) n -> d h n", h=NH)).then_inc(w_loaded, N_DMA)

            def stack(b, g):
                need(sp, st_done, (b - 1) * NS + (g + 1) * GS)
                need(sp, mx_done, (b - 1) * NS + (g + 1) * GS)
                if g == 0:
                    sp.wait_ge(klo_ready, b * NC + NC)
                    sp.wait_ge(qlo_ready, b * NKV * NC + NKV * NC)
                rows = slice(g * DL, (g + 1) * DL)
                for n, part in enumerate((k_hi, k_hi, k_lo)):
                    sp.dma_start(k_stack[n * DL:(n + 1) * DL, g, :].bitcast(F32),
                                 part[rows, :].bitcast(F32)).then_inc(stacked[g * NR], N_DMA)
                for r in range(NR):
                    rows = slice(r * DL, (r + 1) * DL)
                    for n, part in enumerate((q_hi, q_lo, q_hi)):
                        sp.dma_start(q_stack[n * DL:(n + 1) * DL, g * NR + r, :].bitcast(F32),
                                     part[rows, g, :].bitcast(F32)).then_inc(stacked[g * NR + r], N_DMA)

            def slot(k, s):
                b, ls = at(k, s + ROW_LEAD)
                if ls % NBL == 0 and real(b):
                    h = ls // NBL
                    sp.wait_ge(mlo_ready, b * NH + h + 1)
                    for n, part in enumerate((mT_hi, mT_lo)):
                        sp.dma_start(q_stack[MROW + n:MROW + n + 1, h, :].bitcast(F32),
                                     part[:, h, :].bitcast(F32)).then_inc(m_row[h % 2], N_DMA)
                b, ls = at(k, s)
                if real(b):
                    if ls == STACK_1:
                        stack(b, 1)
                    if ls == KEEP:
                        need(sp, x2_ready, b * NC)
                        sp.wait_ge(comb[0], (b + 1) * COMB)
                        sp.dma_start(x1_kept[:], x1[:]).then_inc(kept, N_DMA)

            def front(b, s):
                if s == FRONT:
                    need(sp, comb[0], b * COMB)
                    sp.dma_start(x0[:], x[bass.ds(b, 1)].rearrange("o (t p) d -> p (o t) d", p=P))\
                        .then_inc(x_loaded, N_DMA)
                if s == STACK_0:
                    stack(b, 0)

            def join(b, s):
                pass

            def back(b, s):
                if s == BACK + Y + job_slot(JOBS - 1) + PICK + 2:
                    sp.wait_ge(comb[1], (b + 1) * COMB + CREDIT)
                    sp.dma_start(out[bass.ds(b, 1)].rearrange("o (t p) d -> p (o t) d", p=P), x3[:])\
                        .then_inc(stored, N_DMA)

            timeline(sp, slot, front, join, back)
            sp.wait_ge(stored, NB * N_DMA + CREDIT)

        @block.gpsimd
        def _(pool):
            steps = [0]

            def step(ins):
                ins.then_inc(const_step, 1)
                steps[0] += 1
                pool.wait_ge(const_step, steps[0])

            def select(out, base, pattern, cm, op=ALU.not_equal, fill=1.0):
                step(nc.gpsimd.affine_select(out=out, in_=out, compare_op=op, fill=fill, base=base,
                                             pattern=pattern, channel_multiplier=cm))

            step(nc.gpsimd.memset(ident[:], 0.0))
            select(ident[:], 0, [[-1, P]], 1)
            step(nc.gpsimd.memset(half_power[:], -0.5))
            step(nc.gpsimd.memset(ident_b[:], 0.0))
            select(ident_b[:], 0, [[-1, P]], 1)
            step(nc.gpsimd.memset(mask_qk[:], 0.0))
            select(mask_qk[:], 0, [[-1, P]], 1, ALU.is_ge, MASKED)
            step(nc.gpsimd.memset(mask_kq[:], 0.0))
            select(mask_kq[:], 0, [[1, P]], -1, ALU.is_ge, MASKED)
            assert steps[0] == CONST_STEPS

            def norm_power(b, l):
                pool.wait_ge(stat_step[l], (b + 1) * STAT_STEPS)
                nc.gpsimd.tensor_tensor(rstd[:], var_eps[:], half_power[:], ALU.pow).then_inc(rstd_step[l], 1)
                pool.wait_ge(rstd_step[l], b * 2 + 1)
                nc.gpsimd.tensor_tensor(shift[:], neg_mean[:], rstd[:], ALU.mult).then_inc(rstd_step[l], 1)

            def slot(k, s):
                b, ls = at(k, s + ROW_LEAD)
                if ls % NBL == 0 and real(b):
                    h = ls // NBL
                    pool.wait_ge(mT_ready, b * 2 * NH + 2 * h + 2)
                    nc.gpsimd.tensor_tensor(mT_lo[:, h, :], mT[:, h, :], mT_hi[:, h, :].bitcast(F32),
                                            ALU.subtract).then_inc(mlo_ready, 1)
                b, ls = at(k, s)
                if real(b) and on_pool(ls):
                    w = CH - offset(ls)
                    pool.wait_ge(p_ready, b * NS + ls + 1)
                    nc.gpsimd.tensor_tensor(prob_lo[:, ls % NP, 0:w], prob[:, ls % NP, 0:w],
                                            upper_half(ls, w), ALU.subtract).then_inc(split_done[True], 1)

            def front(b, s):
                if s == FRONT + POWER:
                    norm_power(b, 0)
                if s == LN1 + POWER:
                    norm_power(b, 1)

            def join(b, s):
                pass

            def back(b, s):
                if s == BACK + POWER:
                    norm_power(b, 2)

            timeline(pool, slot, front, join, back)

        @block.scalar
        def _(act):
            def copy(dst, src):
                return nc.scalar.activation(dst, src, ACT.Copy)

            act.wait_ge(w_loaded, 9 * N_DMA)
            copy(we_hi[:], we_sb[:]).then_inc(prep_act, 1)
            copy(down_hi[:], down_sb[:]).then_inc(prep_act, 1)
            act.wait_ge(prep_pe, 1)
            copy(upT[:], bank[0][:, 0:2 * DL]).then_inc(prep_act, 1)
            copy(rw_hi[:], bank[0][:, 2 * DL:2 * DL + NE]).then_inc(prep_act, 1)
            for n in range(2):
                act.wait_ge(prep_pe, 2 + n)
                copy(wqT[:, cols(n)], bank[1 + n][:]).then_inc(prep_act, 1)
            act.wait_ge(prep_pe, 4)
            copy(aq_hi[:], bank[3][:, 0:NH * DL]).then_inc(prep_act, 1)
            act.wait_ge(prep_pe, 5)
            copy(wo_lat[:].rearrange("p g n -> p (g n)"), bank[4][:, 0:NKV * D]).then_inc(prep_act, 1)

            def normalise(b, l, src, c):
                if c == 0:
                    act.wait_ge(rstd_step[l], b * 2 + 2)
                for t in range(c * TC, (c + 1) * TC):
                    nc.scalar.activation(xn[:, t, :], src[:, t, :], ACT.Identity, bias=shift[:, t:t + 1],
                                         scale=rstd[:, t:t + 1]).then_inc(xn_ready[l], 1)

            def high_part(b, l, c):
                if c == 0:
                    if l == 0:
                        need(act, v_done, b)
                        need(act, y_done[1], (b - 2) * JOBS + CREDIT)
                    elif l == 1:
                        act.wait_ge(y_done[0], (b + 1) * JOBS)
                    elif isinstance(b, int):
                        act.wait_ge(v_done, min(b + 3, NB))
                        act.wait_ge(y_done[1], b * JOBS + CREDIT)
                    else:
                        act.wait_ge(v_done, b + 3)
                act.wait_ge(xT_psum[l], b * NC + c + 1)
                copy(xT_hi[:, cols(c)], bank[FB + c][:]).then_inc(xhi_ready[l], 1)

            def norm_piece(b, l, src, n):
                if n in (XN, XN + 1):
                    normalise(b, l, src, n - XN)
                if n in (XT, XT + 1):
                    high_part(b, l, n - XT)

            def gate_exponent(b, f):
                act.wait_ge(gate_step[f], b * GATE_STEPS + 3)
                nc.scalar.activation(g_e[:], g_s[:], ACT.Exp).then_inc(gate_exp[f], 1)

            def slot(k, s):
                b, ls = at(k, s + ROW_LEAD)
                if ls % NBL == 0 and real(b):
                    h = ls // NBL
                    act.wait_ge(mT_psum, b * NH + h + 1)
                    src = bank[MX + ENTRY["row", h if h < NH - 1 else -1] % 2][0:NT, 0:P]
                    copy(mT[:, h, :], src).then_inc(mT_ready, 1)
                    copy(mT_hi[:, h, :], src).then_inc(mT_ready, 1)
                b, ls = at(k, s)
                if real(b):
                    w = CH - offset(ls)
                    act.wait_ge(st_done, b * NS + ls + 1)
                    need(act, pv_done, b * NS + ls - NP + 1)
                    nc.scalar.activation(prob[:, ls % NP, 0:w], bank[ST + ls % NST][:, 0:w], ACT.Exp,
                                         scale=SCALE).then_inc(p_ready, 1)

            def front(b, s):
                norm_piece(b, 0, x0, s - FRONT)
                if s == FRONT + ROUTE:
                    gate_exponent(b, 0)
                norm_piece(b, 1, x1, s - LN1)
                if s == PROJ:
                    for h in range(NH):
                        need(act, stacked[h], b * N_DMA * (6 if h % NR == 0 else 3))
                    for c in range(NC):
                        act.wait_ge(k_done, b * NC + c + 1)
                        copy(k_hi[:, cols(c)], bank[FB + c][0:NKV * DL, :]).then_inc(khi_ready, 1)
                if 1 <= s - PROJ <= NKV * NC:
                    n = s - PROJ - 1
                    g, c = divmod(n, NC)
                    act.wait_ge(q_done, b * NKV * NC + n + 1)
                    copy(q_hi[:, g, cols(c)], bank[FB + (n + 2) % NFB][:]).then_inc(qhi_ready, 1)
                if s == PROJ + NKV * NC + 1:
                    act.wait_ge(v_done, b + 1)
                    need(act, v_step[1], b * 4)
                    copy(v_lat[:].rearrange("p t g l -> p (t g l)"), bank[FB][:]).then_inc(v_ready, 1)

            def join(b, s):
                n = s - JOIN
                if 0 <= n < NKV * NC:
                    g, c = divmod(n, NC)
                    act.wait_ge(yT_psum, b * NKV * NC + n + 1)
                    copy(yT[:, g, cols(c)], bank[FB + n % NFB][:]).then_inc(yT_ready, 1)

            def back(b, s):
                norm_piece(b, 2, x2, s - BACK)
                if s == BACK + ROUTE:
                    gate_exponent(b, 1)

            timeline(act, slot, front, join, back)

        @block.vector
        def _(dve):
            V = nc.vector
            for e in range(NE):
                V.memset(rank[:, e:e + 1], float(NE - e)).then_inc(set_up, 1)
            V.memset(m_part[:], -3e38).then_inc(set_up, 1)
            V.memset(v_parts[:, :, :, VCOLS - 1:VCOLS], 1.0).then_inc(set_up, 1)
            V.memset(k_stack[MROW:KROWS, :, :].bitcast(F32), -1.0).then_inc(set_up, 1)
            V.memset(g_r[:, 0, :], 0.0).then_inc(y_done[1], CREDIT)
            V.memset(g_r[:, 1, :], 0.0).then_inc(comb[1], CREDIT)
            V.memset(g_r[:, 2, :], 0.0).then_inc(stored, CREDIT)

            def low(dst, src, hi):
                return V.tensor_tensor(dst, src, hi.bitcast(F32), ALU.subtract)

            dve.wait_ge(prep_act, 1)
            low(we_lo[:], we_sb[:], we_hi[:]).then_inc(prep_dve, 1)
            dve.wait_ge(prep_act, 2)
            low(down_lo[:], down_sb[:], down_hi[:]).then_inc(prep_dve, 1)
            dve.wait_ge(prep_act, 4)
            low(rw_lo[:], bank[0][:, 2 * DL:2 * DL + NE], rw_hi[:]).then_inc(prep_dve, 1)
            dve.wait_ge(prep_act, 7)
            low(aq_lo[:], bank[3][:, 0:NH * DL], aq_hi[:]).then_inc(prep_dve, 1)
            dve.wait_ge(set_up, NE + 3)
            dve.wait_ge(comb[1], CREDIT)
            dve.wait_ge(y_done[1], CREDIT)
            dve.wait_ge(stored, CREDIT)

            def halves(l, src, tiles):
                for t in tiles:
                    V.bn_stats(stats[:, t, :], src[:, t, :]).then_inc(bn_done[l], 1)

            def statistics(b, l, lo, hi):
                def step(n, op, *args, **kw):
                    if lo <= n < hi:
                        if n == 0:
                            dve.wait_ge(bn_done[l], (b + 1) * NT)
                        else:
                            dve.wait_ge(stat_step[l], b * STAT_STEPS + n)
                        op(*args, **kw).then_inc(stat_step[l], 1)

                mean_e, sq_e, mean_o, sq_o = (stats[:, :, i] for i in (1, 2, 4, 5))
                step(0, V.tensor_tensor, neg_mean[:], mean_e, mean_o, ALU.add)
                step(1, V.tensor_tensor, diff[:], mean_e, mean_o, ALU.subtract)
                step(2, V.tensor_tensor, diff[:], diff[:], diff[:], ALU.mult)
                step(3, V.tensor_tensor, var_eps[:], sq_e, sq_o, ALU.add)
                step(4, V.tensor_scalar, diff[:], diff[:], 0.25, LN_EPS, ALU.mult, ALU.add)
                step(5, V.scalar_tensor_tensor, out=var_eps[:], in0=var_eps[:], scalar=1.0 / D, in1=diff[:],
                     op0=ALU.mult, op1=ALU.add)
                step(6, V.tensor_scalar, neg_mean[:], neg_mean[:], -0.5, None, ALU.mult)

            def low_part(b, l, c):
                dve.wait_ge(xhi_ready[l], b * NC + c + 1)
                low(xT_lo[:, cols(c)], bank[FB + c][:], xT_hi[:, cols(c)]).then_inc(xlo_ready[l], 1)

            def norm_piece(b, l, src, n):
                if l != 1 and n in (0, 1):
                    halves(l, src, range(n * TC, (n + 1) * TC))
                if n == 2:
                    statistics(b, l, 0, 4)
                if n == 3:
                    statistics(b, l, 4, STAT_STEPS)
                if n in (XLO, XLO + 1):
                    low_part(b, l, n - XLO)

            r = [g_r[:, i, :] for i in range(8)]
            rank_b = rank[:].unsqueeze(1).to_broadcast([P, NT, NE])
            bias_b = rb_sb[:].unsqueeze(1).to_broadcast([P, NT, NE])
            logits = bank[FB][:, 0:NT * NE].rearrange("p (t e) -> p t e", t=NT)

            def routing(b, f, lo, hi):
                def step(n, op, *args, **kw):
                    if lo <= n < hi:
                        if n == 0:
                            dve.wait_ge(logits_done[f], b + 1)
                        else:
                            dve.wait_ge(gate_step[f], b * GATE_STEPS + n)
                        if n == 13:
                            dve.wait_ge(gate_exp[f], b + 1)
                        op(*args, **kw).then_inc(gate_step[f], 1)

                step(0, V.tensor_tensor, g_l[:], logits, bias_b, ALU.add)
                step(1, V.reduce_max, r[0], g_l[:], AX.X)
                step(2, V.tensor_tensor, g_s[:], g_l[:], per_expert(r[0]), ALU.subtract)
                step(3, V.scalar_tensor_tensor, out=g_k[:], in0=g_s[:], scalar=0.0, in1=rank_b,
                     op0=ALU.is_ge, op1=ALU.mult)
                step(4, V.reduce_max, r[1], g_k[:], AX.X)
                step(5, V.tensor_tensor, g_1[:], g_k[:], per_expert(r[1]), ALU.is_equal)
                step(6, V.scalar_tensor_tensor, out=g_2[:], in0=g_1[:], scalar=-3e38, in1=g_s[:],
                     op0=ALU.mult, op1=ALU.add)
                step(7, V.reduce_max, r[2], g_2[:], AX.X)
                step(8, V.tensor_tensor, g_k[:], g_2[:], per_expert(r[2]), ALU.is_ge)
                step(9, V.tensor_tensor, g_k[:], g_k[:], rank_b, ALU.mult)
                step(10, V.reduce_max, r[3], g_k[:], AX.X)
                step(11, V.tensor_tensor, g_2[:], g_k[:], per_expert(r[3]), ALU.is_equal)
                step(12, V.tensor_tensor, g_1[:], g_1[:], g_2[:], ALU.add)
                step(13, V.reduce_sum, r[4], g_e[:], AX.X)
                step(14, V.tensor_tensor, g_l[:], g_e[:], g_1[:], ALU.mult)
                step(15, V.reduce_sum, r[5], g_l[:], AX.X)
                step(16, V.scalar_tensor_tensor, out=r[4], in0=r[4], scalar=EPS, in1=r[5],
                     op0=ALU.mult, op1=ALU.add)
                step(17, V.reciprocal, r[4], r[4])
                step(18, V.tensor_tensor, r[5], r[5], r[4], ALU.mult)
                step(19, V.tensor_scalar, r[6], r[5], EPS, 2.0, ALU.max, ALU.mult)
                step(20, V.reciprocal, r[6], r[6])
                step(21, V.tensor_scalar, r[7], r[5], EPS, 1.0, ALU.mult, ALU.add)
                step(22, V.tensor_tensor, r[7], r[7], r[6], ALU.mult)
                step(23, V.tensor_tensor, r[7], r[7], r[4], ALU.mult)
                step(24, V.tensor_tensor, gate[:], g_l[:], per_expert(r[7]), ALU.mult)

            def combine(b, f, j, src, dst):
                t, half = divmod(j, 2)
                done = b * COMB + f * CREDIT + t * TILE_STEPS
                if j == 0:
                    dve.wait_ge(gate_step[f], (b + 1) * GATE_STEPS)
                    if f == 1:
                        dve.wait_ge(stored, b * N_DMA + CREDIT)
                    else:
                        need(dve, kept, b * N_DMA)
                dve.wait_ge(y_done[f], b * JOBS + j + 1 + f * CREDIT)
                for e in range(NE // 2):
                    ee = half * NE // 2 + e
                    if ee >= 2:
                        dve.wait_ge(comb[f], done + ee - 1)
                    y = bank[FB + j % NFB][:, e * D:(e + 1) * D]
                    w = gate[:, t, ee:ee + 1]
                    odd = odd_sum[:, t % 2, :]
                    if ee == 1:
                        ins = V.tensor_scalar(odd, y, w, None, ALU.mult)
                    else:
                        acc = odd if ee % 2 else dst[:, t, :]
                        ins = V.scalar_tensor_tensor(out=acc, in0=y, scalar=w, in1=acc if ee else src[:, t, :],
                                                     op0=ALU.mult, op1=ALU.add)
                    ins.then_inc(comb[f], 1)

            def finish_tile(b, f, t, dst):
                dve.wait_ge(comb[f], b * COMB + f * CREDIT + t * TILE_STEPS + NE)
                V.tensor_tensor(dst[:, t, :], dst[:, t, :], odd_sum[:, t % 2, :], ALU.add).then_inc(comb[f], 1)

            def expert_piece(b, f, n, src, dst):
                if n - PICK in JOB_AT:
                    combine(b, f, JOB_AT[n - PICK], src, dst)
                j = JOB_AT.get(n - PICK - 1)
                if j is not None and j % 2:
                    finish_tile(b, f, j // 2, dst)
                j = JOB_AT.get(n - PICK - 2)
                if j is not None and j % 2 and f == 0:
                    dve.wait_ge(comb[0], b * COMB + (j // 2 + 1) * TILE_STEPS)
                    halves(1, dst, [j // 2])

            def value_parts(b, g):
                part = [v_parts[:, :, g, n * DL:(n + 1) * DL] for n in range(3)]
                if g == 0:
                    dve.wait_ge(v_ready, b + 1)
                need(dve, pv_done, (b - 1) * NS + (g + 1) * GS)
                V.tensor_copy(part[0], v_lat[:, :, g, :]).then_inc(v_step[g], 1)
                dve.wait_ge(v_step[g], b * 4 + 1)
                V.tensor_tensor(v_rest[:], v_lat[:, :, g, :], part[0], ALU.subtract).then_inc(v_step[g], 1)
                dve.wait_ge(v_step[g], b * 4 + 2)
                V.tensor_copy(part[1], v_rest[:]).then_inc(v_step[g], 1)
                dve.wait_ge(v_step[g], b * 4 + 3)
                V.tensor_tensor(part[2], v_rest[:], part[1], ALU.subtract).then_inc(v_step[g], 1)

            def slot(k, s):
                b, ls = at(k, s - NORM_LAG)
                if real(b) and ls in UNIT_ENDS:
                    u = UNIT_ENDS[ls]
                    h, c = divmod(u, NC)
                    dve.wait_ge(pv_done, b * NS + ls + 1)
                    o = bank[OB][:, 0:TC * VCOLS].rearrange("p (t v) -> p t v", t=TC)
                    V.tensor_reduce(out=o_sum[:, u % 2], in_=o[:, :, 0:3 * DL].rearrange("p t (n l) -> p t l n", n=3),
                                    op=ALU.add, axis=AX.X).then_inc(norm_step, 1)
                    V.reciprocal(rden[:, u % 2, :], o[:, :, 3 * DL]).then_inc(norm_step, 1)
                    dve.wait_ge(norm_step, b * 3 * NU + 3 * u + 2)
                    if u == 0:
                        need(dve, yT_psum, b * NKV * NC)
                    V.tensor_tensor(y_lat[:, c * TC:(c + 1) * TC, h, :], o_sum[:, u % 2],
                                    rden[:, u % 2, :].unsqueeze(2).to_broadcast([P, TC, DL]), ALU.mult)\
                        .then_inc(norm_step, 1)
                b, ls = at(k, s + MAX_LEAD - 1)
                if real(b) and ls % NBL == NBL - 1:
                    h = ls // NBL
                    dve.wait_ge(mx_red, b * NS + ls + 1)
                    V.tensor_tensor(m_fin[:, h, :], m_part[:, h, 0, :], m_part[:, h, 1, :],
                                    ALU.max).then_inc(m_merged, 1)
                b, ls = at(k, s + MAX_LEAD)
                if real(b):
                    h, (i, kc) = ls // NBL, MBLOCKS[ls % NBL]
                    w = min(CH, (i + 1) * P - kc * CH)
                    dve.wait_ge(mx_done, b * NS + ls + 1)
                    V.reduce_max(m_part[:, h, kc, i:i + 1], bank[MX + ENTRY["block", ls] % 2][:, 0:w], AX.X).then_inc(mx_red, 1)
                b, ls = at(k, s)
                if real(b) and not on_pool(ls):
                    w = CH - offset(ls)
                    dve.wait_ge(p_ready, b * NS + ls + 1)
                    V.tensor_tensor(prob_lo[:, ls % NP, 0:w], prob[:, ls % NP, 0:w], upper_half(ls, w),
                                    ALU.subtract).then_inc(split_done[False], 1)
                b, ls = at(k, s)
                if real(b) and ls == VPARTS_1:
                    value_parts(b, 1)

            def route_slice(b, f, n):
                per = -(-GATE_STEPS // ROUTE_SLOTS)
                routing(b, f, n * per, min(GATE_STEPS, (n + 1) * per))

            def front(b, s):
                if s == FRONT:
                    dve.wait_ge(x_loaded, (b + 1) * N_DMA)
                norm_piece(b, 0, x0, s - FRONT)
                if 0 <= s - FRONT - ROUTE < ROUTE_SLOTS:
                    route_slice(b, 0, s - FRONT - ROUTE)
                expert_piece(b, 0, s - FRONT - Y, x0, x1)
                norm_piece(b, 1, x1, s - LN1)
                if s == PROJ + 1:
                    for c in range(NC):
                        dve.wait_ge(khi_ready, b * NC + c + 1)
                        low(k_lo[:, cols(c)], bank[FB + c][0:NKV * DL, :], k_hi[:, cols(c)]).then_inc(klo_ready, 1)
                if 2 <= s - PROJ <= NKV * NC + 1:
                    n = s - PROJ - 2
                    g, c = divmod(n, NC)
                    dve.wait_ge(qhi_ready, b * NKV * NC + n + 1)
                    low(q_lo[:, g, cols(c)], bank[FB + (n + 2) % NFB][:], q_hi[:, g, cols(c)]).then_inc(qlo_ready, 1)
                if s == STACK_0:
                    value_parts(b, 0)

            def join(b, s):
                c = s - JOIN - NKV * NC - 1
                if 0 <= c < NC:
                    dve.wait_ge(attn_done, b * NC + c + 1)
                    if c == 0:
                        dve.wait_ge(kept, (b + 1) * N_DMA)
                    tiles = slice(c * TC, (c + 1) * TC)
                    V.tensor_tensor(x2[:, tiles, :], bank[FB + c + 1][:].rearrange("p (t d) -> p t d", t=TC),
                                    x1_kept[:, tiles, :], ALU.add).then_inc(x2_ready, 1)

            def back(b, s):
                if s == BACK:
                    dve.wait_ge(x2_ready, (b + 1) * NC)
                norm_piece(b, 2, x2, s - BACK)
                if 0 <= s - BACK - ROUTE < ROUTE_SLOTS:
                    route_slice(b, 1, s - BACK - ROUTE)
                expert_piece(b, 1, s - BACK - Y, x2, x3)

            timeline(dve, slot, front, join, back)

        @block.tensor
        def _(pe):
            mm = nc.tensor.matmul

            pe.wait_ge(const_step, CONST_STEPS)
            pe.wait_ge(w_loaded, 9 * N_DMA)
            nc.tensor.transpose(bank[0][:, 0:DL], wk_up_sb[:], ident[0:DL, 0:DL])
            nc.tensor.transpose(bank[0][:, DL:2 * DL], wv_up_sb[:], ident[0:DL, 0:DL])
            nc.tensor.transpose(bank[0][:, 2 * DL:2 * DL + NE], rw_sb[:], ident[0:NE, 0:NE]).then_inc(prep_pe, 1)
            for n in range(2):
                for i in range(NH // 2):
                    last = nc.tensor.transpose(bank[1 + n][:, i * P:(i + 1) * P], wq_sb[:, n * NH // 2 + i, :],
                                               ident[:])
                last.then_inc(prep_pe, 1)
            pe.wait_ge(prep_act, 6)
            for h in range(NH):
                last = mm(bank[3][:, h * DL:(h + 1) * DL], wqT[:, h * D:(h + 1) * D], upT[:, 0:DL],
                          start=True, stop=True)
            last.then_inc(prep_pe, 1)
            for h in range(NH):
                g, r = divmod(h, NR)
                last = mm(bank[4][r * DL:(r + 1) * DL, g * D:(g + 1) * D], upT[:, DL:2 * DL], wo_sb[:, h, :],
                          start=True, stop=True)
            last.then_inc(prep_pe, 1)
            pe.wait_ge(prep_act, 8)
            pe.wait_ge(prep_dve, 4)

            def transposes(b, l, c):
                if l == 0 and c == 0:
                    need(pe, comb[1], (b - 2) * COMB + CREDIT)
                    need(pe, v_ready, b)
                    need(pe, qlo_ready, b * NKV * NC)
                    need(pe, x2_ready, (b - 1) * NC)
                if l == 2 and c == 0 and isinstance(b, int):
                    need(pe, comb[1], b * COMB + CREDIT)
                    pe.wait_ge(x2_ready, (b + 1) * NC)
                if l == 2 and c == 0 and not isinstance(b, int):
                    pe.wait_ge(v_ready, b + 3)
                    pe.wait_ge(qlo_ready, (b + 3) * NKV * NC)
                pe.wait_ge(xn_ready[l], b * NT + (c + 1) * TC)
                for i in range(TC):
                    last = nc.tensor.transpose(bank[FB + c][:, i * P:(i + 1) * P], xn[:, c * TC + i, :], ident[:])
                last.then_inc(xT_psum[l], 1)

            def three(dst, lhs, rhs):
                mm(dst, lhs[0], rhs[0], start=True, stop=False)
                mm(dst, lhs[0], rhs[1], start=False, stop=False)
                return mm(dst, lhs[1], rhs[0], start=False, stop=True)

            def both(hi, lo, *at):
                return hi[at], lo[at]

            def x_part(t):
                return both(xT_hi, xT_lo, slice(None), slice(t * P, (t + 1) * P))

            def router(b, f, l):
                pe.wait_ge(xlo_ready[l], (b + 1) * NC)
                for t in range(NT):
                    last = three(bank[FB][:, t * NE:(t + 1) * NE], x_part(t), (rw_hi[:], rw_lo[:]))
                last.then_inc(logits_done[f], 1)

            def expert_products(b, f, j):
                t, half = divmod(j, 2)
                if j >= NFB:
                    t0, half0 = divmod(j - NFB, 2)
                    pe.wait_ge(comb[f], b * COMB + f * CREDIT + t0 * TILE_STEPS + (half0 + 1) * NE // 2)
                elif j == 0:
                    pe.wait_ge(gate_step[f], b * GATE_STEPS + 1)
                three(bank[FB + j % NFB][:], x_part(t), both(we_hi, we_lo, slice(None), cols(half)))\
                    .then_inc(y_done[f], 1)

            def bank_of(b, entry):
                n = ENTRY[entry]
                what, i = ENTRIES[(n - 2) % len(ENTRIES)]
                before = b - 1 if n < 2 else b
                if what == "block":
                    need(pe, mx_red, before * NS + i + 1)
                else:
                    need(pe, mT_ready, (before * NH + i + 1) * 2)
                return bank[MX + n % 2]

            def maximum(b, ls):
                h, (i, kc) = ls // NBL, MBLOCKS[ls % NBL]
                w = min(CH, (i + 1) * P - kc * CH)
                diagonal = kc == i // TC
                if ls % NBL == 0:
                    pe.wait_ge(stacked[h], (b + 1) * N_DMA * (6 if h % NR == 0 else 3))
                into = bank_of(b, ("block", ls))
                last = mm(into[:, 0:w], q_stack[0:MROW, h, i * P:(i + 1) * P],
                          k_stack[0:MROW, h // NR, kc * CH:kc * CH + w], start=True, stop=not diagonal)
                if diagonal:
                    last = mm(into[:, w - P:w], ident_b[:], mask_qk[:], start=False, stop=True)
                last.then_inc(mx_done, 1)

            def scores(b, ls):
                h, (c, j) = ls // NBL, BLOCKS[ls % NBL]
                off = offset(ls)
                w = CH - off
                diagonal = j >= TC * c
                if ls % NBL == 0:
                    pe.wait_ge(m_row[h % 2], (b * NH // 2 + h // 2 + 1) * 2 * N_DMA)
                need(pe, p_ready, b * NS + ls - NST + 1)
                last = mm(bank[ST + ls % NST][:, 0:w], k_stack[:, h // NR, j * P:(j + 1) * P],
                          q_stack[:, h, c * CH + off:(c + 1) * CH], start=True, stop=not diagonal)
                if diagonal:
                    last = mm(bank[ST + ls % NST][:, 0:P], ident_b[:], mask_kq[:], start=False, stop=True)
                last.then_inc(st_done, 1)

            def values(b, ls):
                h, (c, j) = ls // NBL, BLOCKS[ls % NBL]
                off = offset(ls)
                w = CH - off
                first, final = j == 0, ls in UNIT_ENDS
                if ls % GS == 0:
                    pe.wait_ge(v_step[ls // GS], (b + 1) * 4)
                mine = on_pool(ls)
                pe.wait_ge(split_done[mine], b * splits(NS - 1, mine) + splits(ls, mine))
                if first:
                    need(pe, norm_step, (b * NU + h * NC + c) * 3)
                v = v_parts[:, j, h // NR, 0:VCOLS]
                hi = upper_half(ls, w)
                for n, i in enumerate(range(off // P, TC)):
                    acc = bank[OB][:, i * VCOLS:(i + 1) * VCOLS]
                    mm(acc, hi[:, n * P:(n + 1) * P], v, start=first and i == 0, stop=False, skip_group_check=True)
                    last = mm(acc, prob_lo[:, ls % NP, n * P:(n + 1) * P], v, start=False,
                              stop=final and i == TC - 1, skip_group_check=True)
                last.then_inc(pv_done, 1)

            def slot(k, s):
                b, ls = at(k, s + ROW_LEAD)
                if ls % NBL == 0 and real(b):
                    h = ls // NBL
                    pe.wait_ge(m_merged, b * NH + h + 1)
                    if h < NH - 1:
                        into = bank_of(b, ("row", h))
                    elif isinstance(b, int) and b == NB - 1:
                        into = bank[MX + ENTRY["row", -1] % 2]
                    else:
                        into = bank_of(b + 1, ("row", -1))
                    nc.tensor.transpose(into[0:NT, 0:P], m_fin[:, h, :], ident[:]).then_inc(mT_psum, 1)
                b, ls = at(k, s)
                if real(b):
                    scores(b, ls)
                b, ls = at(k, s + MAX_LEAD)
                if real(b):
                    maximum(b, ls)
                for back_by in range(PV_LAG + PV_HOLD, PV_LAG - 1, -1):
                    b, ls = at(k, s - back_by)
                    if real(b) and values_slot(ls) == ls + back_by:
                        values(b, ls)

            def norm_piece(b, l, n):
                if n in (XT, XT + 1):
                    transposes(b, l, n - XT)

            def front(b, s):
                norm_piece(b, 0, s - FRONT)
                if s == FRONT + LOGITS:
                    router(b, 0, 0)
                if s - FRONT - Y in JOB_AT:
                    expert_products(b, 0, JOB_AT[s - FRONT - Y])
                norm_piece(b, 1, s - LN1)
                nk = NKV * DL
                if s == PROJ:
                    pe.wait_ge(xlo_ready[1], (b + 1) * NC)
                    for c in range(NC):
                        three(bank[FB + c][0:nk, :], (down_hi[:, 0:nk], down_lo[:, 0:nk]),
                              both(xT_hi, xT_lo, slice(None), cols(c))).then_inc(k_done, 1)
                if 1 <= s - PROJ <= NKV * NC:
                    n = s - PROJ - 1
                    g, c = divmod(n, NC)
                    if n in (1, 2):
                        pe.wait_ge(klo_ready, b * NC + n)
                    elif n == 3:
                        pe.wait_ge(qlo_ready, b * NKV * NC + 1)
                    three(bank[FB + (n + 2) % NFB][:], both(aq_hi, aq_lo, slice(None), slice(g * P, (g + 1) * P)),
                          both(xT_hi, xT_lo, slice(None), cols(c))).then_inc(q_done, 1)
                if s == PROJ + NKV * NC + 1:
                    pe.wait_ge(qlo_ready, b * NKV * NC + 2)
                    for t in range(NT):
                        last = three(bank[FB][:, t * nk:(t + 1) * nk], x_part(t), (down_hi[:, nk:], down_lo[:, nk:]))
                    last.then_inc(v_done, 1)

            def join(b, s):
                n = s - JOIN
                if n == 0:
                    pe.wait_ge(norm_step, (b + 1) * NU * 3)
                    need(pe, comb[1], b * COMB + CREDIT)
                if 0 <= n < NKV * NC:
                    g, c = divmod(n, NC)
                    if n == NFB:
                        pe.wait_ge(yT_ready, b * NKV * NC + 1)
                    for i in range(TC):
                        last = nc.tensor.transpose(bank[FB + n % NFB][:, i * P:(i + 1) * P],
                                                   y_lat[:, c * TC + i, g * NR:(g + 1) * NR, :]
                                                   .rearrange("p r l -> p (r l)"), ident[:])
                    last.then_inc(yT_psum, 1)
                if n == NKV * NC:
                    pe.wait_ge(yT_ready, (b + 1) * NKV * NC)
                    for c in range(NC):
                        for i in range(TC):
                            t = c * TC + i
                            for g in range(NKV):
                                last = mm(bank[FB + c + 1][:, i * D:(i + 1) * D], yT[:, g, t * P:(t + 1) * P],
                                          wo_lat[:, g, :], start=g == 0, stop=g == NKV - 1)
                        last.then_inc(attn_done, 1)

            def back(b, s):
                norm_piece(b, 2, s - BACK)
                if s == BACK + LOGITS:
                    router(b, 1, 2)
                if s - BACK - Y in JOB_AT:
                    expert_products(b, 1, JOB_AT[s - BACK - Y])

            timeline(pe, slot, front, join, back)


_INS = ["L0_attn_x", "L0_attn_wq", "L0_attn_wk_down", "L0_attn_wv_down", "L0_attn_wk_up", "L0_attn_wv_up",
        "L0_attn_wo", "L0_ffn_router_w", "L0_ffn_router_b", "L0_ffn_expert_weights"]


def kernel(**inputs):
    import numpy as np
    import concourse.bacc as bacc
    from concourse.bass_utils import run_bass_kernel_spmd

    nc = bacc.Bacc("TRN2", target_bir_lowering=False, num_devices=1)
    arrays, args = {}, []
    for name in _INS:
        a = np.ascontiguousarray(inputs[name])
        arrays[f"in_{name}"] = a
        args.append(nc.dram_tensor(f"in_{name}", a.shape, mybir.dt.from_np(a.dtype), kind="ExternalInput").ap())
    out = nc.dram_tensor("out_x", (NB, T, D), F32, kind="ExternalOutput").ap()
    macaron(nc, *args, out)
    r = run_bass_kernel_spmd(nc, [arrays], core_ids=[0])
    return np.asarray(r.results[0]["out_x"])
```

```python
from contextlib import ExitStack

import concourse.bass as bass
from concourse import mybir

F32 = mybir.dt.float32
F32R = mybir.dt.float32r
BF16 = mybir.dt.bfloat16
FP16 = mybir.dt.float16
ALU = mybir.AluOpType
ACT = mybir.ActivationFunctionType
AX = mybir.AxisListType

NB, T, D = 4, 1024, 128
P = 128
NT = T // P
CH = 512
NC = T // CH
TC = CH // P
NE = 8
NH, NKV, DL = 8, 2, 32
NR = NH // NKV
NU = NH * NC
SCALE = float(D) ** -0.5
LN_EPS = 1e-5
EPS = 1e-10
MASKED = -1e30

MROW = 3 * DL
KROWS = MROW + 2
VCOLS = 3 * DL + 1

BLOCKS = [(c, j) for c in range(NC) for j in range(TC * (c + 1))]
MBLOCKS = [(i, k) for i in range(NT) for k in range(i // TC + 1)]
NBL = len(BLOCKS)
NS = NH * NBL
GS = NS // NKV

MAX_LEAD = 20
ROW_LEAD = 6
PV_LAG = 5
PV_HOLD = 2
NORM_LAG = PV_LAG + 1
NP = 9

NMX, NST, NFB = 3, 2, 2
MX, ST, OB, FB = 0, NMX, NMX + NST, NMX + NST + 1

CUT = 4
JOIN = 7
JOIN_OUT = 11
OUT_STEP = 1
KEEP = 11
STACK_1 = 5
STACK_EVERY = 2
VALUES_1 = 10
BN = [8, 0, 42]
STATS = [10, 55, 45]
POWER = [12, 55, 47]
XN = [13, 59, 49]
XT = [16, 62, 52]
XHI = [17, 63, 52]
XLO = [17, 64, 53]
XT_STEP = 2
LOGITS = [21, 57]
LOGITS_STEP = [0, 0]
ROUTE = [22, 59]
ROUTE_SLOTS = [3, 10]
GATE_EXP = [24, 58]
Y = [26, 74]
PACE = [3, 3]
PICK_ACT = 1
PICK_DVE = 1
SPREAD = 0
FINISH = 2
TILE_STATS = 4
LOAD = 4
PROJ = 68
QUERIES = 69
VALUES = 74
STACK_0 = QUERIES + 3
VALUES_STEP = 0
VALUES_0 = VALUES + 2

HALF = NE // 2
STAT_SLOTS = 2
STAT_STEPS = 7
GATE_STEPS = 26
N_DMA = 16
JOBS = 2 * NT
CONST_STEPS = 9


def last_block(u):
    h, c = divmod(u, NC)
    return h * NBL + (TC - 1 if c == 0 else NBL - 1)


UNIT_ENDS = {last_block(u): u for u in range(NU)}


def offset(s):
    c, j = BLOCKS[s % NBL]
    return max(0, j - TC * c) * P


def diagonal(s):
    c, j = BLOCKS[s % NBL]
    return j >= TC * c


def on_pool(s):
    return s % NBL not in (0, 3, 6)


def splits(s, pool):
    return sum(on_pool(i) == pool for i in range(s + 1))


def values_slot(s):
    n = BLOCKS[s % NBL][1]
    return s + max(0, PV_HOLD - n) + PV_LAG


def job_slot(f, j):
    return Y[f] + j // 2 * PACE[f] + j % 2 * (PACE[f] // 2)


def job_at(f, s):
    return next((j for j in range(JOBS) if job_slot(f, j) == s), None)


ENTRIES = []
for _m in range(NS):
    if _m % NBL == MAX_LEAD - NBL - ROW_LEAD:
        ENTRIES.append(("row", _m // NBL - 1))
    ENTRIES.append(("block", _m))
ENTRY = {e: n for n, e in enumerate(ENTRIES)}


def maxima_bank(entry):
    return MX + ENTRY[entry] % NMX


def entry_before(entry):
    n = ENTRY[entry]
    for back_by in range(1, len(ENTRIES)):
        other = ENTRIES[(n - back_by) % len(ENTRIES)]
        if maxima_bank(other) == maxima_bank(entry):
            return other, back_by > n


def at(k, s):
    return k + s // NS if s // NS else k, s % NS


def real(b):
    return not isinstance(b, int) or 0 <= b < NB


def is_first(b):
    return isinstance(b, int) and b == 0


def job_banks(b, f):
    alone = isinstance(b, int) and b == (NB - 1 if f else 0)
    return [FB, FB + 1, MX, MX + 1] if alone else [FB, FB + 1]


def job_bank(b, f, j):
    banks = job_banks(b, f)
    return banks[j % len(banks)]


def need(engine, semaphore, value):
    if not isinstance(value, int) or value > 0:
        engine.wait_ge(semaphore, value)


def timeline(engine, slot, front, join, back):
    for s in range(CUT, CUT + NS):
        front(0, s)

    def run(k, lo, hi):
        for s in range(lo, hi):
            slot(k, s)
            if s >= CUT:
                if real(k - 1):
                    join(k - 1, s)
                if real(k + 1):
                    front(k + 1, s)
                if real(k - 1):
                    back(k - 1, s)

    run(0, -MAX_LEAD, CUT + NS)
    with engine.Fori(1, NB - 1) as k:
        run(k, CUT, CUT + NS)
    run(NB - 1, CUT, CUT + NS)
    for s in range(CUT, CUT + NS):
        slot(NB, s)
        join(NB - 1, s)
        back(NB - 1, s)


def macaron(nc, x, wq, wk_down, wv_down, wk_up, wv_up, wo, router_w, router_b, experts, out):
    ctx = ExitStack()
    with ctx:
        def sb(name, shape, dt=F32):
            return ctx.enter_context(nc.sbuf_tensor(name, shape, dt))

        def sem(name):
            return ctx.enter_context(nc.semaphore(name))

        def sems(name, n):
            return [sem(f"{name}{i}") for i in range(n)]

        bank = [ctx.enter_context(nc.psum_tensor(f"bank{i}", [P, CH], F32)) for i in range(8)]

        ident = sb("ident", [P, P])
        ident_b = sb("ident_b", [P, P], BF16)
        mask_qk = sb("mask_qk", [P, P], BF16)
        mask_kq = sb("mask_kq", [P, P], BF16)
        rank = sb("rank", [P, NE])
        half_power = sb("half_power", [P, NT])
        wk_up_sb = sb("wk_up_sb", [DL, D])
        wv_up_sb = sb("wv_up_sb", [DL, D])
        down_sb = sb("down_sb", [P, 2 * NKV * DL])
        rw_sb = sb("rw_sb", [NE, D])
        rb_sb = sb("rb_sb", [P, NE])
        we_sb = sb("we_sb", [P, NE * D])
        upT = sb("upT", [P, 2 * DL])
        aq_hi = sb("aq_hi", [P, NH * DL], F32R)
        aq_lo = sb("aq_lo", [P, NH * DL], F32R)
        down_hi = sb("down_hi", [P, 2 * NKV * DL], F32R)
        down_lo = sb("down_lo", [P, 2 * NKV * DL], F32R)
        we_hi = sb("we_hi", [P, NE * D], F32R)
        we_lo = sb("we_lo", [P, NE * D], F32R)
        rw_parts = sb("rw_parts", [P, 2 * NE], F32R)
        wo_lat = sb("wo_lat", [P, NKV, D])
        x0 = sb("x0", [P, NT, D])
        x1 = sb("x1", [P, NT, D])
        x1_kept = sb("x1_kept", [P, NT, D])
        x2 = sb("x2", [P, NT, D])
        x3 = sb("x3", [P, NT, D])
        wq_sb, wqT, wo_sb = x3, x1_kept, x2
        stats = sb("stats", [P, 3, NT, 6])
        neg_mean = sb("neg_mean", [P, 3, NT])
        diff = sb("diff", [P, 3, NT])
        var_eps = sb("var_eps", [P, 3, NT])
        rstd = sb("rstd", [P, 3, NT])
        shift = sb("shift", [P, 3, NT])
        xn = sb("xn", [P, NT, D])
        xT_hi = sb("xT_hi", [P, 2, T], F32R)
        xT_lo = sb("xT_lo", [P, 2, T], F32R)
        g_l = sb("g_l", [P, NT, NE])
        g_s = sb("g_s", [P, NT, NE])
        g_e = sb("g_e", [P, NT, NE])
        g_k = sb("g_k", [P, NT, NE])
        g_1 = sb("g_1", [P, NT, NE])
        g_2 = sb("g_2", [P, NT, NE])
        g_r = sb("g_r", [P, 8, NT])
        gate = sb("gate", [P, 2, NT, NE])
        scaled = sb("scaled", [P, 2, HALF, D])
        dve_sum = sb("dve_sum", [P, 2, 3, D])
        pair_sum = sb("pair_sum", [P, 2, 2, D])
        q_hi = sb("q_hi", [P, NKV, T], F32R)
        q_lo = sb("q_lo", [P, NKV, T], F32R)
        k_hi = sb("k_hi", [NKV * DL, T], F32R)
        k_lo = sb("k_lo", [NKV * DL, T], F32R)
        q_stack = sb("q_stack", [KROWS, NH, T], F32R)
        k_stack = sb("k_stack", [KROWS, NKV, T], F32R)
        v_lat = sb("v_lat", [P, NT, NKV, DL])
        v_parts = sb("v_parts", [P, NT, NKV, VCOLS + 1], BF16)
        v_rest = sb("v_rest", [P, NT, DL])
        m_part = sb("m_part", [P, NH, 2, NT])
        m_fin = sb("m_fin", [P, NH, NT])
        mT = sb("mT", [NT, NH, P])
        mT_hi = sb("mT_hi", [NT, NH, P], F32R)
        mT_lo = sb("mT_lo", [NT, NH, P], F32R)
        prob = sb("prob", [P, NP, CH])
        prob_lo = sb("prob_lo", [P, NP, CH], FP16)
        o_sum = sb("o_sum", [P, 2, TC, DL])
        rden = sb("rden", [P, 2, TC])
        y_lat = sb("y_lat", [P, NT, NH, DL])
        yT = sb("yT", [P, NKV, T])

        small_loaded = sem("small_loaded")
        we_loaded = sem("we_loaded")
        rb_loaded = sem("rb_loaded")
        wq_loaded = sem("wq_loaded")
        wo_loaded = sem("wo_loaded")
        const_step = sem("const_step")
        set_up = sem("set_up")
        prep_pe = sem("prep_pe")
        prep_act = sem("prep_act")
        prep_dve = sem("prep_dve")
        x_loaded = sem("x_loaded")
        bn_done = sems("bn_done", 3)
        stat_step = sems("stat_step", 3)
        rstd_step = sems("rstd_step", 3)
        xn_ready = sems("xn_ready", 3)
        xT_psum = sems("xT_psum", 3)
        xhi_ready = sems("xhi_ready", 3)
        xlo_ready = sems("xlo_ready", 3)
        logits_done = sems("logits_done", 2)
        gate_step = sems("gate_step", 2)
        gate_exp = sems("gate_exp", 2)
        y_done = sems("y_done", 2)
        act_picked = sems("act_picked", 2)
        dve_picked = sems("dve_picked", 2)
        pair_step = sems("pair_step", 2)
        tile_done = sems("tile_done", 2)
        stored = sem("stored")
        kept = sem("kept")
        q_done = sem("q_done")
        k_done = sem("k_done")
        v_done = sem("v_done")
        qhi_ready = sem("qhi_ready")
        qlo_ready = sem("qlo_ready")
        khi_ready = sem("khi_ready")
        klo_ready = sem("klo_ready")
        v_ready = sem("v_ready")
        v_step = sems("v_step", NKV)
        stacked = sems("stacked", NH)
        mx_done = sem("mx_done")
        mx_red = sem("mx_red")
        m_merged = sem("m_merged")
        mT_psum = sem("mT_psum")
        mT_ready = sem("mT_ready")
        mlo_ready = sem("mlo_ready")
        m_row = sems("m_row", 2)
        st_done = sem("st_done")
        p_ready = sem("p_ready")
        split_done = {True: sem("split_pool"), False: sem("split_dve")}
        pv_done = sem("pv_done")
        norm_step = sem("norm_step")
        yT_psum = sem("yT_psum")
        yT_ready = sem("yT_ready")
        attn_done = sem("attn_done")
        x2_ready = sem("x2_ready")
        CREDIT = 1

        def per_expert(ap):
            return ap.unsqueeze(2).to_broadcast([P, NT, NE])

        def upper_half(s, w):
            return prob[:, s % NP, :].bitcast(BF16)[:, 1:2 * w:2]

        def cols(c):
            return slice(c * CH, (c + 1) * CH)

        def others_tiles(b, f):
            if f == 0:
                return (b - 2) * NT + CREDIT
            return min(b + 3, NB) * NT if isinstance(b, int) else (b + 3) * NT

        block = ctx.enter_context(nc.Block())

        @block.sync
        def _(sp):
            sp.dma_start(x0[:], x[bass.ds(0, 1)].rearrange("o (t p) d -> p (o t) d", p=P))\
                .then_inc(x_loaded, N_DMA)
            sp.dma_start(rw_sb[:], router_w).then_inc(small_loaded, N_DMA)
            sp.dma_start(wk_up_sb[:], wk_up).then_inc(small_loaded, N_DMA)
            sp.dma_start(wv_up_sb[:], wv_up).then_inc(small_loaded, N_DMA)
            sp.dma_start(down_sb[:, 0:NKV * DL], wk_down).then_inc(small_loaded, N_DMA)
            sp.dma_start(down_sb[:, NKV * DL:], wv_down).then_inc(small_loaded, N_DMA)
            sp.dma_start(we_sb[:].rearrange("h (e d) -> h e d", e=NE),
                         experts.rearrange("e h d -> h e d")).then_inc(we_loaded, N_DMA)
            sp.dma_start(rb_sb[:], router_b.unsqueeze(0).to_broadcast([P, NE])).then_inc(rb_loaded, N_DMA)
            sp.dma_start(wq_sb[:], wq.rearrange("m (h d) -> m h d", h=NH)).then_inc(wq_loaded, N_DMA)
            sp.dma_start(wo_sb[:], wo.rearrange("(h d) n -> d h n", h=NH)).then_inc(wo_loaded, N_DMA)

            def stack(b, g, n):
                if n:
                    r = n - 1
                    rows = slice(r * DL, (r + 1) * DL)
                    for i, part in enumerate((q_hi, q_lo, q_hi)):
                        sp.dma_start(q_stack[i * DL:(i + 1) * DL, g * NR + r, :].bitcast(F32),
                                     part[rows, g, :].bitcast(F32)).then_inc(stacked[g * NR + r], N_DMA)
                    return
                if g == 0:
                    sp.wait_ge(qlo_ready, b * NKV * NC + NC)
                else:
                    sp.wait_ge(st_done, b * NS + 1)
                rows = slice(g * DL, (g + 1) * DL)
                for i, part in enumerate((k_hi, k_hi, k_lo)):
                    sp.dma_start(k_stack[i * DL:(i + 1) * DL, g, :].bitcast(F32),
                                 part[rows, :].bitcast(F32)).then_inc(stacked[g * NR], N_DMA)

            def slot(k, s):
                b, ls = at(k, s + ROW_LEAD)
                if ls % NBL == 0 and real(b):
                    h = ls // NBL
                    sp.wait_ge(mlo_ready, b * NH + h + 1)
                    for n, part in enumerate((mT_hi, mT_lo)):
                        sp.dma_start(q_stack[MROW + n:MROW + n + 1, h, :].bitcast(F32),
                                     part[:, h, :].bitcast(F32)).then_inc(m_row[h % 2], N_DMA)
                b, ls = at(k, s)
                if real(b):
                    for n in range(NR + 1):
                        if ls == STACK_1 + n * STACK_EVERY:
                            stack(b, 1, n)
                    if ls == KEEP:
                        need(sp, x2_ready, b * NC)
                        sp.wait_ge(tile_done[0], (b + 1) * NT)
                        sp.dma_start(x1_kept[:], x1[:]).then_inc(kept, N_DMA)

            def front(b, s):
                for n in range(NR + 1):
                    if s == STACK_0 + max(0, n - 1) * STACK_EVERY:
                        stack(b, 0, n)

            def join(b, s):
                pass

            def back(b, s):
                if s == job_slot(1, JOBS - 1) + FINISH + 1:
                    tokens = out[bass.ds(b, 1)].rearrange("o (t p) d -> p (o t) d", p=P)
                    sp.wait_ge(tile_done[1], (b + 1) * NT + CREDIT)
                    sp.dma_start(tokens, x3[:]).then_inc(stored, N_DMA)

            timeline(sp, slot, front, join, back)
            sp.wait_ge(stored, NB * N_DMA + CREDIT)

        @block.gpsimd
        def _(pool):
            steps = [0]

            def step(ins):
                ins.then_inc(const_step, 1)
                steps[0] += 1
                pool.wait_ge(const_step, steps[0])

            def select(out, base, pattern, cm, op=ALU.not_equal, fill=1.0):
                step(nc.gpsimd.affine_select(out=out, in_=out, compare_op=op, fill=fill, base=base,
                                             pattern=pattern, channel_multiplier=cm))

            step(nc.gpsimd.memset(ident[:], 0.0))
            select(ident[:], 0, [[-1, P]], 1)
            step(nc.gpsimd.memset(half_power[:], -0.5))
            step(nc.gpsimd.memset(ident_b[:], 0.0))
            select(ident_b[:], 0, [[-1, P]], 1)
            step(nc.gpsimd.memset(mask_qk[:], 0.0))
            select(mask_qk[:], 0, [[-1, P]], 1, ALU.is_ge, MASKED)
            step(nc.gpsimd.memset(mask_kq[:], 0.0))
            select(mask_kq[:], 0, [[1, P]], -1, ALU.is_ge, MASKED)
            assert steps[0] == CONST_STEPS

            def norm_power(b, l):
                pool.wait_ge(stat_step[l], (b + 1) * STAT_STEPS)
                nc.gpsimd.tensor_tensor(rstd[:, l], var_eps[:, l], half_power[:], ALU.pow).then_inc(rstd_step[l], 1)
                pool.wait_ge(rstd_step[l], b * 2 + 1)
                nc.gpsimd.tensor_tensor(shift[:, l], neg_mean[:, l], rstd[:, l], ALU.mult).then_inc(rstd_step[l], 1)

            def finish_tile(b, f, t, dst):
                if t == 0:
                    if f == 1:
                        pool.wait_ge(stored, b * N_DMA + CREDIT)
                    else:
                        need(pool, kept, b * N_DMA)
                pair = pair_sum[:, t % 2]
                step = b * 2 * NT + 2 * t
                pool.wait_ge(dve_picked[f], (b * NT + t + 1) * HALF)
                nc.gpsimd.tensor_tensor(pair, dve_sum[:, t % 2, 1:3], scaled[:, t % 2, 2:4], ALU.add)\
                    .then_inc(pair_step[f], 1)
                pool.wait_ge(pair_step[f], step + 1)
                nc.gpsimd.tensor_tensor(pair[:, 0], pair[:, 0], pair[:, 1], ALU.add).then_inc(pair_step[f], 1)
                pool.wait_ge(pair_step[f], step + 2)
                nc.gpsimd.tensor_tensor(dst[:, t, :], pair[:, 0], dve_sum[:, t % 2, 0], ALU.add)\
                    .then_inc(tile_done[f], 1)

            def expert_piece(b, f, s, dst):
                j = job_at(f, s - FINISH)
                if j is not None and j % 2:
                    finish_tile(b, f, j // 2, dst)

            def slot(k, s):
                b, ls = at(k, s + ROW_LEAD)
                if ls % NBL == 0 and real(b):
                    h = ls // NBL
                    pool.wait_ge(mT_ready, b * 2 * NH + 2 * h + 2)
                    nc.gpsimd.tensor_tensor(mT_lo[:, h, :], mT[:, h, :], mT_hi[:, h, :].bitcast(F32),
                                            ALU.subtract).then_inc(mlo_ready, 1)
                b, ls = at(k, s)
                if real(b) and on_pool(ls):
                    w = CH - offset(ls)
                    pool.wait_ge(p_ready, b * NS + ls + 1)
                    nc.gpsimd.tensor_tensor(prob_lo[:, ls % NP, 0:w], prob[:, ls % NP, 0:w],
                                            upper_half(ls, w), ALU.subtract).then_inc(split_done[True], 1)

            def front(b, s):
                if s == POWER[0]:
                    norm_power(b, 0)
                if s == POWER[1]:
                    norm_power(b, 1)
                expert_piece(b, 0, s, x1)

            def join(b, s):
                pass

            def back(b, s):
                if s == POWER[2]:
                    norm_power(b, 2)
                expert_piece(b, 1, s, x3)

            timeline(pool, slot, front, join, back)

        @block.scalar
        def _(act):
            def copy(dst, src):
                return nc.scalar.activation(dst, src, ACT.Copy)

            def prepare_first():
                act.wait_ge(prep_pe, 1)
                copy(upT[:], bank[0][:, 0:2 * DL]).then_inc(prep_act, 1)
                copy(rw_parts[:, 0:NE], bank[0][:, 2 * DL:2 * DL + NE]).then_inc(prep_act, 1)
                copy(down_hi[:], down_sb[:]).then_inc(prep_act, 1)
                act.wait_ge(we_loaded, N_DMA)
                copy(we_hi[:], we_sb[:]).then_inc(prep_act, 1)
                for n in range(2):
                    act.wait_ge(prep_pe, 2 + n)
                    copy(wqT[:, n * TC:(n + 1) * TC, :].rearrange("p h d -> p (h d)"), bank[1 + n][:]).then_inc(prep_act, 1)

            def prepare_rest():
                act.wait_ge(prep_pe, 4)
                copy(aq_hi[:], bank[3][:, 0:NH * DL]).then_inc(prep_act, 1)
                act.wait_ge(prep_pe, 5)
                copy(wo_lat[:].rearrange("p g n -> p (g n)"), bank[4][:, 0:NKV * D]).then_inc(prep_act, 1)

            prepare_first()

            def normalise(b, l, src, n):
                if n == 0:
                    act.wait_ge(rstd_step[l], b * 2 + 2)
                    if l == 0:
                        need(act, xT_psum[1], b * NC)
                    elif l == 1:
                        act.wait_ge(xT_psum[0], (b + 1) * NC)
                        need(act, xT_psum[2], (b - 1) * NC)
                    else:
                        act.wait_ge(xT_psum[0], min(b + 3, NB) * NC if isinstance(b, int) else (b + 3) * NC)
                        act.wait_ge(xT_psum[1], min(b + 2, NB) * NC if isinstance(b, int) else (b + 2) * NC)
                for t in range(2 * n, 2 * n + 2):
                    nc.scalar.activation(xn[:, t, :], src[:, t, :], ACT.Identity, bias=shift[:, l, t:t + 1],
                                         scale=rstd[:, l, t:t + 1]).then_inc(xn_ready[l], 1)

            def high_part(b, l, c):
                if c == 0:
                    if l == 0:
                        need(act, v_done, b)
                    elif l == 1:
                        act.wait_ge(y_done[0], (b + 1) * JOBS)
                    else:
                        act.wait_ge(y_done[1], b * JOBS + CREDIT)
                act.wait_ge(xT_psum[l], b * NC + c + 1)
                copy(xT_hi[:, l // 2, cols(c)], bank[FB + c][:]).then_inc(xhi_ready[l], 1)

            def norm_piece(b, l, src, s):
                if 0 <= s - XN[l] < NT // 2:
                    normalise(b, l, src, s - XN[l])
                if s - XHI[l] in (0, XT_STEP):
                    high_part(b, l, (s - XHI[l]) // XT_STEP)

            def expert_piece(b, f, s):
                j = job_at(f, s - PICK_ACT)
                if j is None or j % 2:
                    return
                t = j // 2
                if t == 0:
                    act.wait_ge(gate_step[f], (b + 1) * GATE_STEPS)
                    need(act, tile_done[1 - f], others_tiles(b, f))
                if t < 2:
                    need(act, tile_done[f], b * NT + f * CREDIT)
                else:
                    act.wait_ge(tile_done[f], b * NT + t - 1 + f * CREDIT)
                act.wait_ge(y_done[f], b * JOBS + j + 1 + f * CREDIT)
                for i in range(HALF):
                    nc.scalar.activation(scaled[:, t % 2, i, :], bank[job_bank(b, f, j)][:, i * D:(i + 1) * D],
                                         ACT.Copy, scale=gate[:, f, t, i:i + 1])\
                        .then_inc(act_picked[f], 1)

            def gate_exponent(b, f):
                act.wait_ge(gate_step[f], b * GATE_STEPS + 4)
                nc.scalar.activation(g_e[:], g_s[:], ACT.Exp).then_inc(gate_exp[f], 1)

            def slot(k, s):
                b, ls = at(k, s + ROW_LEAD)
                if ls % NBL == 0 and real(b):
                    h = ls // NBL
                    act.wait_ge(mT_psum, b * NH + h + 1)
                    src = bank[maxima_bank(("row", h if h < NH - 1 else -1))][0:NT, 0:P]
                    copy(mT[:, h, :], src).then_inc(mT_ready, 1)
                    copy(mT_hi[:, h, :], src).then_inc(mT_ready, 1)
                b, ls = at(k, s)
                if real(b):
                    w = CH - offset(ls)
                    act.wait_ge(st_done, b * NS + ls + 1)
                    need(act, pv_done, b * NS + ls - NP + 1)
                    nc.scalar.activation(prob[:, ls % NP, 0:w], bank[ST + ls % NST][:, 0:w], ACT.Exp,
                                         scale=SCALE).then_inc(p_ready, 1)

            def front(b, s):
                if s == LOAD and not is_first(b):
                    act.dma_start(x0[:], x[bass.ds(b, 1)].rearrange("o (t p) d -> p (o t) d", p=P))\
                        .then_inc(x_loaded, N_DMA)
                norm_piece(b, 0, x0, s)
                if s == GATE_EXP[0]:
                    gate_exponent(b, 0)
                    if is_first(b):
                        prepare_rest()
                expert_piece(b, 0, s)
                norm_piece(b, 1, x1, s)
                if s == PROJ:
                    for h in range(NH):
                        need(act, stacked[h], b * N_DMA * (6 if h % NR == 0 else 3))
                    for c in range(NC):
                        act.wait_ge(k_done, b * NC + c + 1)
                        copy(k_hi[:, cols(c)], bank[FB + c][0:NKV * DL, :]).then_inc(khi_ready, 1)
                if 0 <= s - QUERIES < NKV * NC:
                    n = s - QUERIES
                    g, c = divmod(n, NC)
                    act.wait_ge(q_done, b * NKV * NC + n + 1)
                    copy(q_hi[:, g, cols(c)], bank[FB + n % NFB][:]).then_inc(qhi_ready, 1)
                if s == VALUES:
                    act.wait_ge(v_done, b + 1)
                    need(act, v_step[1], b * 4)
                    copy(v_lat[:].rearrange("p t g l -> p (t g l)"), bank[FB][:]).then_inc(v_ready, 1)

            def join(b, s):
                n = s - JOIN
                if 0 <= n < NKV * NC:
                    g, c = divmod(n, NC)
                    act.wait_ge(yT_psum, b * NKV * NC + n + 1)
                    copy(yT[:, g, cols(c)], bank[FB + n % NFB][:]).then_inc(yT_ready, 1)

            def back(b, s):
                norm_piece(b, 2, x2, s)
                if s == GATE_EXP[1]:
                    gate_exponent(b, 1)
                expert_piece(b, 1, s)

            timeline(act, slot, front, join, back)

        @block.vector
        def _(dve):
            V = nc.vector
            for e in range(NE):
                V.memset(rank[:, e:e + 1], float(NE - e)).then_inc(set_up, 1)
            V.memset(m_part[:], -3e38).then_inc(set_up, 1)
            V.memset(v_parts[:, :, :, VCOLS - 1:VCOLS], 1.0).then_inc(set_up, 1)
            V.memset(k_stack[MROW:KROWS, :, :].bitcast(F32), -1.0).then_inc(set_up, 1)
            V.memset(g_r[:, 0, :], 0.0).then_inc(y_done[1], CREDIT)
            V.memset(g_r[:, 1, :], 0.0).then_inc(tile_done[1], CREDIT)
            V.memset(g_r[:, 2, :], 0.0).then_inc(stored, CREDIT)

            def low(dst, src, hi):
                return V.tensor_tensor(dst, src, hi.bitcast(F32), ALU.subtract)

            def prepare_first():
                dve.wait_ge(prep_act, 2)
                low(rw_parts[:, NE:2 * NE], bank[0][:, 2 * DL:2 * DL + NE], rw_parts[:, 0:NE]).then_inc(prep_dve, 1)
                dve.wait_ge(prep_act, 3)
                low(down_lo[:], down_sb[:], down_hi[:]).then_inc(prep_dve, 1)
                dve.wait_ge(prep_act, 4)
                low(we_lo[:], we_sb[:], we_hi[:]).then_inc(prep_dve, 1)
                dve.wait_ge(rb_loaded, N_DMA)

            def prepare_rest():
                dve.wait_ge(prep_act, 7)
                low(aq_lo[:], bank[3][:, 0:NH * DL], aq_hi[:]).then_inc(prep_dve, 1)

            dve.wait_ge(set_up, NE + 3)
            dve.wait_ge(tile_done[1], CREDIT)
            dve.wait_ge(y_done[1], CREDIT)
            dve.wait_ge(stored, CREDIT)

            def halves(l, src, tiles):
                for t in tiles:
                    V.bn_stats(stats[:, l, t, :], src[:, t, :]).then_inc(bn_done[l], 1)

            def statistics(b, l, lo, hi):
                def step(n, op, *args, **kw):
                    if lo <= n < hi:
                        if n == 0:
                            dve.wait_ge(bn_done[l], (b + 1) * NT)
                        else:
                            dve.wait_ge(stat_step[l], b * STAT_STEPS + n)
                        op(*args, **kw).then_inc(stat_step[l], 1)

                mean_e, sq_e, mean_o, sq_o = (stats[:, l, :, i] for i in (1, 2, 4, 5))
                step(0, V.tensor_tensor, neg_mean[:, l], mean_e, mean_o, ALU.add)
                step(1, V.tensor_tensor, diff[:, l], mean_e, mean_o, ALU.subtract)
                step(2, V.tensor_tensor, diff[:, l], diff[:, l], diff[:, l], ALU.mult)
                step(3, V.tensor_tensor, var_eps[:, l], sq_e, sq_o, ALU.add)
                step(4, V.tensor_scalar, diff[:, l], diff[:, l], 0.25, LN_EPS, ALU.mult, ALU.add)
                step(5, V.scalar_tensor_tensor, out=var_eps[:, l], in0=var_eps[:, l], scalar=1.0 / D, in1=diff[:, l],
                     op0=ALU.mult, op1=ALU.add)
                step(6, V.tensor_scalar, neg_mean[:, l], neg_mean[:, l], -0.5, None, ALU.mult)

            def low_part(b, l, c):
                dve.wait_ge(xhi_ready[l], b * NC + c + 1)
                low(xT_lo[:, l // 2, cols(c)], bank[FB + c][:], xT_hi[:, l // 2, cols(c)]).then_inc(xlo_ready[l], 1)

            def norm_piece(b, l, src, s):
                if l != 1 and s - BN[l] in (0, 1):
                    halves(l, src, range((s - BN[l]) * TC, (s - BN[l] + 1) * TC))
                if s - XLO[l] in (0, XT_STEP):
                    low_part(b, l, (s - XLO[l]) // XT_STEP)

            r = [g_r[:, i, :] for i in range(8)]
            rank_b = rank[:].unsqueeze(1).to_broadcast([P, NT, NE])
            bias_b = rb_sb[:].unsqueeze(1).to_broadcast([P, NT, NE])
            logits = bank[FB][:, 0:NT * 2 * NE].rearrange("p (t e) -> p t e", t=NT)

            def routing(b, f, lo, hi):
                def step(n, after, op, *args, **kw):
                    if lo <= n < hi:
                        if n == 0:
                            dve.wait_ge(logits_done[f], b + 1)
                        else:
                            dve.wait_ge(gate_step[f], b * GATE_STEPS + after + 1)
                        if n == 9:
                            dve.wait_ge(gate_exp[f], b + 1)
                        op(*args, **kw).then_inc(gate_step[f], 1)

                step(0, None, V.tensor_tensor, g_l[:], logits[:, :, 0:NE], bias_b, ALU.add)
                step(1, 0, V.tensor_tensor, g_l[:], logits[:, :, NE:2 * NE], g_l[:], ALU.add)
                step(2, 1, V.reduce_max, r[0], g_l[:], AX.X)
                step(3, 2, V.tensor_tensor, g_s[:], g_l[:], per_expert(r[0]), ALU.subtract)
                step(4, 3, V.scalar_tensor_tensor, out=g_k[:], in0=g_s[:], scalar=0.0, in1=rank_b,
                     op0=ALU.is_ge, op1=ALU.mult)
                step(5, 4, V.reduce_max, r[1], g_k[:], AX.X)
                step(6, 5, V.tensor_tensor, g_1[:], g_k[:], per_expert(r[1]), ALU.is_equal)
                step(7, 6, V.scalar_tensor_tensor, out=g_2[:], in0=g_1[:], scalar=-3e38, in1=g_s[:],
                     op0=ALU.mult, op1=ALU.add)
                step(8, 7, V.reduce_max, r[2], g_2[:], AX.X)
                step(9, 7, V.reduce_sum, r[4], g_e[:], AX.X)
                step(10, 8, V.tensor_tensor, g_k[:], g_2[:], per_expert(r[2]), ALU.is_ge)
                step(11, 10, V.tensor_tensor, g_k[:], g_k[:], rank_b, ALU.mult)
                step(12, 11, V.reduce_max, r[3], g_k[:], AX.X)
                step(13, 12, V.tensor_tensor, g_2[:], g_k[:], per_expert(r[3]), ALU.is_equal)
                step(14, 13, V.tensor_tensor, g_1[:], g_1[:], g_2[:], ALU.add)
                step(15, 14, V.tensor_tensor, g_l[:], g_e[:], g_1[:], ALU.mult)
                step(16, 15, V.reduce_sum, r[5], g_l[:], AX.X)
                step(17, 16, V.scalar_tensor_tensor, out=r[4], in0=r[4], scalar=EPS, in1=r[5],
                     op0=ALU.mult, op1=ALU.add)
                step(18, 17, V.reciprocal, r[4], r[4])
                step(19, 18, V.tensor_tensor, r[5], r[5], r[4], ALU.mult)
                step(20, 19, V.tensor_scalar, r[6], r[5], EPS, 2.0, ALU.max, ALU.mult)
                step(21, 19, V.tensor_scalar, r[7], r[5], EPS, 1.0, ALU.mult, ALU.add)
                step(22, 20, V.reciprocal, r[6], r[6])
                step(23, 21, V.tensor_tensor, r[7], r[7], r[4], ALU.mult)
                step(24, 23, V.tensor_tensor, r[7], r[7], r[6], ALU.mult)
                step(25, 24, V.tensor_tensor, gate[:, f], g_l[:], per_expert(r[7]), ALU.mult)

            def combine(b, f, j, src, experts):
                t = j // 2
                if experts[0] == 0:
                    if t == 0:
                        dve.wait_ge(gate_step[f], (b + 1) * GATE_STEPS)
                        need(dve, tile_done[1 - f], others_tiles(b, f))
                    if t < 2:
                        need(dve, tile_done[f], b * NT + f * CREDIT)
                    else:
                        dve.wait_ge(tile_done[f], b * NT + t - 1 + f * CREDIT)
                    dve.wait_ge(y_done[f], b * JOBS + j + 1 + f * CREDIT)
                sums = [dve_sum[:, t % 2, i, :] for i in range(3)]
                addends = [src[:, t, :], scaled[:, t % 2, 0, :], scaled[:, t % 2, 1, :], sums[0]]
                for e in experts:
                    if e == 1:
                        dve.wait_ge(act_picked[f], (b * NT + t + 1) * HALF)
                    if e == HALF - 1:
                        dve.wait_ge(dve_picked[f], (b * NT + t) * HALF + 1)
                    V.scalar_tensor_tensor(out=sums[e % 3], in0=bank[job_bank(b, f, j)][:, e * D:(e + 1) * D],
                                           scalar=gate[:, f, t, HALF + e:HALF + e + 1], in1=addends[e],
                                           op0=ALU.mult, op1=ALU.add).then_inc(dve_picked[f], 1)

            def expert_piece(b, f, s, src, dst):
                for n in range(2):
                    j = job_at(f, s - PICK_DVE - n * SPREAD)
                    if j is not None and j % 2:
                        combine(b, f, j, src, (2 * n, 2 * n + 1))
                j = job_at(f, s - PICK_DVE - TILE_STATS)
                if j is not None and j % 2 and f == 0:
                    dve.wait_ge(tile_done[0], b * NT + j // 2 + 1)
                    halves(1, dst, [j // 2])

            def chains(b, layers, norms, s, part):
                for f in layers:
                    n, parts = (s - ROUTE[f]) * 3 + part, ROUTE_SLOTS[f] * 3
                    if 0 <= n < parts:
                        routing(b, f, GATE_STEPS * n // parts, GATE_STEPS * (n + 1) // parts)
                for l in norms:
                    n, parts = (s - STATS[l]) * 3 + part, STAT_SLOTS * 3
                    if 0 <= n < parts:
                        statistics(b, l, STAT_STEPS * n // parts, STAT_STEPS * (n + 1) // parts)

            def slot(k, s):
                def chained(part):
                    if s >= CUT and real(k + 1):
                        chains(k + 1, (0,), (0, 1), s, part)
                    if s >= CUT and real(k - 1):
                        chains(k - 1, (1,), (2,), s, part)

                chained(0)
                unit = None
                b, ls = at(k, s - NORM_LAG)
                if real(b) and ls in UNIT_ENDS:
                    unit, of = UNIT_ENDS[ls], b
                    dve.wait_ge(pv_done, b * NS + ls + 1)
                    o = bank[OB][:, 0:TC * VCOLS].rearrange("p (t v) -> p t v", t=TC)
                    V.reciprocal(rden[:, unit % 2, :], o[:, :, 3 * DL]).then_inc(norm_step, 1)
                    V.tensor_reduce(out=o_sum[:, unit % 2], in_=o[:, :, 0:3 * DL].rearrange("p t (n l) -> p t l n", n=3),
                                    op=ALU.add, axis=AX.X).then_inc(norm_step, 1)
                chained(1)
                b, ls = at(k, s + MAX_LEAD - 1)
                if real(b) and ls % NBL == NBL - 1:
                    h = ls // NBL
                    dve.wait_ge(mx_red, b * NS + ls + 1)
                    V.tensor_tensor(m_fin[:, h, :], m_part[:, h, 0, :], m_part[:, h, 1, :],
                                    ALU.max).then_inc(m_merged, 1)
                b, ls = at(k, s + MAX_LEAD)
                if real(b):
                    h, (i, kc) = ls // NBL, MBLOCKS[ls % NBL]
                    w = min(CH, (i + 1) * P - kc * CH)
                    dve.wait_ge(mx_done, b * NS + ls + 1)
                    V.reduce_max(m_part[:, h, kc, i:i + 1], bank[maxima_bank(("block", ls))][:, 0:w], AX.X)\
                        .then_inc(mx_red, 1)
                if unit is not None:
                    h, c = divmod(unit, NC)
                    dve.wait_ge(norm_step, of * 3 * NU + 3 * unit + 2)
                    if unit == 0:
                        need(dve, yT_psum, of * NKV * NC)
                    V.tensor_tensor(y_lat[:, c * TC:(c + 1) * TC, h, :], o_sum[:, unit % 2],
                                    rden[:, unit % 2, :].unsqueeze(2).to_broadcast([P, TC, DL]), ALU.mult)\
                        .then_inc(norm_step, 1)
                chained(2)
                b, ls = at(k, s)
                if real(b) and not on_pool(ls):
                    w = CH - offset(ls)
                    dve.wait_ge(p_ready, b * NS + ls + 1)
                    V.tensor_tensor(prob_lo[:, ls % NP, 0:w], prob[:, ls % NP, 0:w], upper_half(ls, w),
                                    ALU.subtract).then_inc(split_done[False], 1)
                if real(b) and 0 <= ls - VALUES_1 < 4:
                    value_parts(b, 1, ls - VALUES_1)

            def value_parts(b, g, n):
                part = [v_parts[:, :, g, i * DL:(i + 1) * DL] for i in range(3)]
                if n == 0:
                    if g == 0:
                        dve.wait_ge(v_ready, b + 1)
                    need(dve, pv_done, (b - 1) * NS + (g + 1) * GS)
                    V.tensor_copy(part[0], v_lat[:, :, g, :]).then_inc(v_step[g], 1)
                else:
                    dve.wait_ge(v_step[g], b * 4 + n)
                if n == 1:
                    V.tensor_tensor(v_rest[:], v_lat[:, :, g, :], part[0], ALU.subtract).then_inc(v_step[g], 1)
                if n == 2:
                    V.tensor_copy(part[1], v_rest[:]).then_inc(v_step[g], 1)
                if n == 3:
                    V.tensor_tensor(part[2], v_rest[:], part[1], ALU.subtract).then_inc(v_step[g], 1)

            def front(b, s):
                if s == BN[0]:
                    dve.wait_ge(x_loaded, (b + 1) * N_DMA)
                norm_piece(b, 0, x0, s)
                if is_first(b):
                    for part in range(3):
                        chains(b, (0,), (0, 1), s, part)
                if is_first(b) and s == POWER[0]:
                    prepare_first()
                expert_piece(b, 0, s, x0, x1)
                if is_first(b) and s == POWER[1]:
                    prepare_rest()
                norm_piece(b, 1, x1, s)
                if s == PROJ + 1:
                    for c in range(NC):
                        dve.wait_ge(khi_ready, b * NC + c + 1)
                        low(k_lo[:, cols(c)], bank[FB + c][0:NKV * DL, :], k_hi[:, cols(c)]).then_inc(klo_ready, 1)
                if 1 <= s - QUERIES <= NKV * NC:
                    n = s - QUERIES - 1
                    g, c = divmod(n, NC)
                    dve.wait_ge(qhi_ready, b * NKV * NC + n + 1)
                    if n == NC - 1:
                        need(dve, st_done, (b - 1) * NS + GS)
                    low(q_lo[:, g, cols(c)], bank[FB + n % NFB][:], q_hi[:, g, cols(c)]).then_inc(qlo_ready, 1)
                if 0 <= s - VALUES_0 < 4:
                    value_parts(b, 0, s - VALUES_0)

            def join(b, s):
                if s - JOIN_OUT - 1 in (0, OUT_STEP):
                    c = (s - JOIN_OUT - 1) // OUT_STEP
                    dve.wait_ge(attn_done, b * NC + c + 1)
                    if c == 0:
                        dve.wait_ge(kept, (b + 1) * N_DMA)
                    tiles = slice(c * TC, (c + 1) * TC)
                    V.tensor_tensor(x2[:, tiles, :], bank[FB + c][:].rearrange("p (t d) -> p t d", t=TC),
                                    x1_kept[:, tiles, :], ALU.add).then_inc(x2_ready, 1)

            def back(b, s):
                if s == BN[2]:
                    dve.wait_ge(x2_ready, (b + 1) * NC)
                norm_piece(b, 2, x2, s)
                expert_piece(b, 1, s, x2, x3)

            timeline(dve, slot, front, join, back)

        @block.tensor
        def _(pe):
            mm = nc.tensor.matmul

            def prepare_first():
                pe.wait_ge(const_step, CONST_STEPS)
                pe.wait_ge(small_loaded, 5 * N_DMA)
                nc.tensor.transpose(bank[0][:, 0:DL], wk_up_sb[:], ident[0:DL, 0:DL])
                nc.tensor.transpose(bank[0][:, DL:2 * DL], wv_up_sb[:], ident[0:DL, 0:DL])
                nc.tensor.transpose(bank[0][:, 2 * DL:2 * DL + NE], rw_sb[:], ident[0:NE, 0:NE])\
                    .then_inc(prep_pe, 1)

            def prepare_queries():
                pe.wait_ge(wq_loaded, N_DMA)
                for n in range(2):
                    for i in range(NH // 2):
                        last = nc.tensor.transpose(bank[1 + n][:, i * P:(i + 1) * P], wq_sb[:, n * NH // 2 + i, :],
                                                   ident[:])
                    last.then_inc(prep_pe, 1)
                pe.wait_ge(prep_act, 6)
                for h in range(NH):
                    last = mm(bank[3][:, h * DL:(h + 1) * DL], wqT[:, h, :], upT[:, 0:DL],
                              start=True, stop=True)
                last.then_inc(prep_pe, 1)

            def prepare_rest():
                pe.wait_ge(wo_loaded, N_DMA)
                for h in range(NH):
                    g, r = divmod(h, NR)
                    last = mm(bank[4][r * DL:(r + 1) * DL, g * D:(g + 1) * D], upT[:, DL:2 * DL], wo_sb[:, h, :],
                              start=True, stop=True)
                last.then_inc(prep_pe, 1)

            prepare_first()
            prepare_queries()

            def layer_read(f, batches):
                need(pe, dve_picked[f], batches * NT * HALF)
                need(pe, act_picked[f], batches * NT * HALF)

            def transposes(b, l, c):
                if l == 0 and c == 0:
                    need(pe, v_ready, b)
                    need(pe, qlo_ready, b * NKV * NC)
                    need(pe, x2_ready, (b - 1) * NC)
                if l == 1 and c == 0:
                    need(pe, gate_step[1], (b - 2) * GATE_STEPS + 2)
                if l == 2 and c == 0:
                    layer_read(0, min(b + 3, NB) if isinstance(b, int) else b + 3)
                    pe.wait_ge(x2_ready, (b + 1) * NC)
                pe.wait_ge(xn_ready[l], b * NT + (c + 1) * TC)
                for i in range(TC):
                    last = nc.tensor.transpose(bank[FB + c][:, i * P:(i + 1) * P], xn[:, c * TC + i, :], ident[:])
                last.then_inc(xT_psum[l], 1)

            def three(dst, lhs, rhs):
                mm(dst, lhs[0], rhs[0], start=True, stop=False)
                mm(dst, lhs[0], rhs[1], start=False, stop=False)
                return mm(dst, lhs[1], rhs[0], start=False, stop=True)

            def both(hi, lo, *at):
                return hi[at], lo[at]

            def x_part(f, t):
                return both(xT_hi, xT_lo, slice(None), f, slice(t * P, (t + 1) * P))

            def router(b, f, l, c):
                if c == 0:
                    pe.wait_ge(xlo_ready[l], (b + 1) * NC)
                for t in range(c * TC, (c + 1) * TC):
                    hi, lo = x_part(f, t)
                    into = bank[FB][:, t * 2 * NE:(t + 1) * 2 * NE]
                    mm(into, hi, rw_parts[:], start=t == 0, stop=False, skip_group_check=True)
                    last = mm(into[:, 0:NE], lo, rw_parts[:, 0:NE], start=False, stop=t == NT - 1,
                              skip_group_check=True)
                if c == NC - 1:
                    last.then_inc(logits_done[f], 1)

            def expert_products(b, f, j):
                t, half = divmod(j, 2)
                ring = len(job_banks(b, f))
                if j >= ring:
                    t, half = divmod(j - ring, 2)
                    pe.wait_ge(dve_picked[f] if half else act_picked[f], (b * NT + t + 1) * HALF)
                    t, half = divmod(j, 2)
                elif j == 0:
                    pe.wait_ge(gate_step[f], b * GATE_STEPS + 2)
                    if f == 1:
                        batches = min(b + 3, NB) if isinstance(b, int) else b + 3
                        pe.wait_ge(v_ready, batches)
                        pe.wait_ge(qlo_ready, batches * NKV * NC)
                three(bank[job_bank(b, f, j)][:], x_part(f, t), both(we_hi, we_lo, slice(None), cols(half)))\
                    .then_inc(y_done[f], 1)

            def bank_of(b, entry):
                (what, i), in_last = entry_before(entry)
                before = b - 1 if in_last else b
                if what == "block":
                    need(pe, mx_red, before * NS + i + 1)
                else:
                    need(pe, mT_ready, (before * NH + i + 1) * 2)
                return bank[maxima_bank(entry)]

            def maximum(b, ls):
                h, (i, kc) = ls // NBL, MBLOCKS[ls % NBL]
                w = min(CH, (i + 1) * P - kc * CH)
                diagonal = kc == i // TC
                if ls % NBL == 0:
                    pe.wait_ge(stacked[h], (b + 1) * N_DMA * (6 if h % NR == 0 else 3))
                into = bank_of(b, ("block", ls))
                last = mm(into[:, 0:w], q_stack[0:MROW, h, i * P:(i + 1) * P],
                          k_stack[0:MROW, h // NR, kc * CH:kc * CH + w], start=True, stop=not diagonal)
                if diagonal:
                    last = mm(into[:, w - P:w], ident_b[:], mask_qk[:], start=False, stop=True)
                last.then_inc(mx_done, 1)

            def scores(b, ls):
                h, (c, j) = ls // NBL, BLOCKS[ls % NBL]
                off = offset(ls)
                if ls % NBL == 0:
                    pe.wait_ge(m_row[h % 2], (b * NH // 2 + h // 2 + 1) * 2 * N_DMA)
                    if h == 0:
                        pe.wait_ge(qlo_ready, (b + 1) * NKV * NC)
                need(pe, p_ready, b * NS + ls - NST + 1)
                last = mm(bank[ST + ls % NST][:, 0:CH - off], k_stack[:, h // NR, j * P:(j + 1) * P],
                          q_stack[:, h, c * CH + off:(c + 1) * CH], start=True, stop=not diagonal(ls))
                if diagonal(ls):
                    last = mm(bank[ST + ls % NST][:, 0:P], ident_b[:], mask_kq[:], start=False, stop=True)
                last.then_inc(st_done, 1)

            def values(b, ls):
                h, (c, j) = ls // NBL, BLOCKS[ls % NBL]
                off = offset(ls)
                w = CH - off
                first, final = j == 0, ls in UNIT_ENDS
                if ls % GS == 0:
                    pe.wait_ge(v_step[ls // GS], (b + 1) * 4)
                mine = on_pool(ls)
                pe.wait_ge(split_done[mine], b * splits(NS - 1, mine) + splits(ls, mine))
                if first:
                    need(pe, norm_step, (b * NU + h * NC + c) * 3)
                v = v_parts[:, j, h // NR, 0:VCOLS]
                hi = upper_half(ls, w)
                for n, i in enumerate(range(off // P, TC)):
                    acc = bank[OB][:, i * VCOLS:(i + 1) * VCOLS]
                    mm(acc, hi[:, n * P:(n + 1) * P], v, start=first and i == 0, stop=False, skip_group_check=True)
                    last = mm(acc, prob_lo[:, ls % NP, n * P:(n + 1) * P], v, start=False,
                              stop=final and i == TC - 1, skip_group_check=True)
                last.then_inc(pv_done, 1)

            def slot(k, s):
                b, ls = at(k, s + ROW_LEAD)
                if ls % NBL == 0 and real(b):
                    h = ls // NBL
                    pe.wait_ge(m_merged, b * NH + h + 1)
                    if h < NH - 1:
                        into = bank_of(b, ("row", h))
                    elif isinstance(b, int) and b == NB - 1:
                        into = bank[maxima_bank(("row", -1))]
                    else:
                        into = bank_of(b + 1, ("row", -1))
                    nc.tensor.transpose(into[0:NT, 0:P], m_fin[:, h, :], ident[:]).then_inc(mT_psum, 1)
                b, ls = at(k, s)
                if real(b):
                    scores(b, ls)
                b, ls = at(k, s + MAX_LEAD)
                if real(b):
                    maximum(b, ls)
                for back_by in range(PV_LAG + PV_HOLD, PV_LAG - 1, -1):
                    b, ls = at(k, s - back_by)
                    if real(b) and values_slot(ls) == ls + back_by:
                        values(b, ls)

            def norm_piece(b, l, s):
                if s - XT[l] in (0, XT_STEP):
                    transposes(b, l, (s - XT[l]) // XT_STEP)

            def front(b, s):
                norm_piece(b, 0, s)
                for c in range(NC):
                    if s == LOGITS[0] + c * LOGITS_STEP[0]:
                        if is_first(b) and c == 0:
                            pe.wait_ge(prep_dve, 3)
                        router(b, 0, 0, c)
                        if is_first(b) and c == NC - 1:
                            prepare_rest()
                if job_at(0, s) is not None:
                    expert_products(b, 0, job_at(0, s))
                norm_piece(b, 1, s)
                nk = NKV * DL
                if s == PROJ:
                    if is_first(b):
                        pe.wait_ge(prep_act, 8)
                        pe.wait_ge(prep_dve, 4)
                    pe.wait_ge(xlo_ready[1], (b + 1) * NC)
                    for c in range(NC):
                        three(bank[FB + c][0:nk, :], (down_hi[:, 0:nk], down_lo[:, 0:nk]),
                              both(xT_hi, xT_lo, slice(None), 0, cols(c))).then_inc(k_done, 1)
                if 0 <= s - QUERIES < NKV * NC:
                    n = s - QUERIES
                    g, c = divmod(n, NC)
                    if n < NC:
                        pe.wait_ge(klo_ready, b * NC + n + 1)
                    else:
                        pe.wait_ge(qlo_ready, b * NKV * NC + n - 1)
                    three(bank[FB + n % NFB][:], both(aq_hi, aq_lo, slice(None), slice(g * P, (g + 1) * P)),
                          both(xT_hi, xT_lo, slice(None), 0, cols(c))).then_inc(q_done, 1)
                for c in range(NC):
                    if s != VALUES - (NC - 1 - c) * VALUES_STEP:
                        continue
                    if c == 0:
                        pe.wait_ge(qlo_ready, b * NKV * NC + 3)
                    for t in range(c * TC, (c + 1) * TC):
                        last = three(bank[FB][:, t * nk:(t + 1) * nk], x_part(0, t), (down_hi[:, nk:], down_lo[:, nk:]))
                    if c == NC - 1:
                        last.then_inc(v_done, 1)

            def join(b, s):
                n = s - JOIN
                if n == 0:
                    pe.wait_ge(norm_step, (b + 1) * NU * 3)
                    need(pe, tile_done[1], b * NT + CREDIT)
                    pe.wait_ge(v_ready, min(b + 2, NB) if isinstance(b, int) else b + 2)
                    pe.wait_ge(qlo_ready, (min(b + 2, NB) if isinstance(b, int) else b + 2) * NKV * NC)
                if 0 <= n < NKV * NC:
                    g, c = divmod(n, NC)
                    if n >= NFB:
                        pe.wait_ge(yT_ready, b * NKV * NC + n - NFB + 1)
                    for i in range(TC):
                        last = nc.tensor.transpose(bank[FB + n % NFB][:, i * P:(i + 1) * P],
                                                   y_lat[:, c * TC + i, g * NR:(g + 1) * NR, :]
                                                   .rearrange("p r l -> p (r l)"), ident[:])
                    last.then_inc(yT_psum, 1)
                if s - JOIN_OUT in (0, OUT_STEP):
                    c = (s - JOIN_OUT) // OUT_STEP
                    if c == 0:
                        pe.wait_ge(yT_ready, (b + 1) * NKV * NC)
                    for i in range(TC):
                        t = c * TC + i
                        for g in range(NKV):
                            last = mm(bank[FB + c][:, i * D:(i + 1) * D], yT[:, g, t * P:(t + 1) * P],
                                      wo_lat[:, g, :], start=g == 0, stop=g == NKV - 1)
                    last.then_inc(attn_done, 1)

            def back(b, s):
                norm_piece(b, 2, s)
                for c in range(NC):
                    if s == LOGITS[1] + c * LOGITS_STEP[1]:
                        router(b, 1, 2, c)
                if job_at(1, s) is not None:
                    expert_products(b, 1, job_at(1, s))

            timeline(pe, slot, front, join, back)


_INS = ["L0_attn_x", "L0_attn_wq", "L0_attn_wk_down", "L0_attn_wv_down", "L0_attn_wk_up", "L0_attn_wv_up",
        "L0_attn_wo", "L0_ffn_router_w", "L0_ffn_router_b", "L0_ffn_expert_weights"]


def kernel(**inputs):
    import numpy as np
    import concourse.bacc as bacc
    from concourse.bass_utils import run_bass_kernel_spmd

    nc = bacc.Bacc("TRN2", target_bir_lowering=False, num_devices=1)
    arrays, args = {}, []
    for name in _INS:
        a = np.ascontiguousarray(inputs[name])
        arrays[f"in_{name}"] = a
        args.append(nc.dram_tensor(f"in_{name}", a.shape, mybir.dt.from_np(a.dtype), kind="ExternalInput").ap())
    out = nc.dram_tensor("out_x", (NB, T, D), F32, kind="ExternalOutput").ap()
    macaron(nc, *args, out)
    r = run_bass_kernel_spmd(nc, [arrays], core_ids=[0])
    return np.asarray(r.results[0]["out_x"])
```
